# Optimizing a Trainium2 kernel written in Bass

```python
import numpy as np
import jax
import jax.numpy as jnp

def _softmax(x, axis=-1):
    return jax.nn.softmax(x, axis=axis)

def _gelu(x):
    return jax.nn.gelu(x, approximate=True)

def _silu(x):
    return jax.nn.silu(x)

def _sigmoid(x):
    return jax.nn.sigmoid(x)

def _layernorm(x, axis=-1, eps=1e-05):
    m = jnp.mean(x, axis=axis, keepdims=True)
    v = jnp.var(x, axis=axis, keepdims=True)
    return (x - m) / jnp.sqrt(v + eps)

def _scatter_add(tgt, idx, src, axis=0):
    return tgt.at[idx].add(src)

def _segment_sum(src, seg, n):
    return jax.ops.segment_sum(src, seg, n)
kernel_name = 'mk_adj_preln_d1_adj_r2_390dd9'

def setup_inputs(seed: int=0):
    np.random.seed(seed)
    _w = jnp.asarray

    def _rec_inputs():
        import jax
        import jax.numpy as jnp
        _gk = jax.random.key(seed)
        x = -0.0002928 + 1 * jax.random.normal(jax.random.fold_in(_gk, 1), (3327, 512), jnp.float32)
        _a = jax.random.bernoulli(jax.random.fold_in(_gk, 2), 0.00120228, (3327, 3327))
        _a = jnp.logical_or(_a, jnp.swapaxes(_a, -1, -2))
        _a = jnp.logical_or(_a, jnp.eye(3327, dtype=bool))
        _af = _a.astype(jnp.float32)
        _af = _af * jax.random.uniform(jax.random.fold_in(_gk, 3), (3327, 3327), jnp.float32, 0.05, 1)
        adj = _af
        return (x, adj)
    x, adj = _rec_inputs()

    def _L0_gnn_setup():
        import jax, jax.numpy as jnp
        import numpy as np
        D_IN, D_ATTN, STEPS = (512, 64, 2)
        P_TOP, TAU, LN_EPS = (0.9, 1.0, 1e-05)
        N = 2048

        def _xavier(key, shape):
            fan_in, fan_out = (shape[0], shape[1])
            lim = jnp.sqrt(6.0 / (fan_in + fan_out))
            return jax.random.uniform(key, shape, jnp.float32, -lim, lim)

        def _adj_from_feats(Xa, W1, W2, W3):
            Q = Xa @ W1
            K = Xa @ W3
            logits = Q @ W2 @ K.T / TAU
            n = logits.shape[1]
            order = jnp.argsort(-logits, axis=1)
            vals = jnp.take_along_axis(logits, order, axis=1)
            probs = jax.nn.softmax(vals, axis=1)
            csum = jnp.cumsum(probs, axis=1)
            k_i = jnp.sum(csum < P_TOP, axis=1) + 1
            keep = jnp.arange(n)[None, :] < k_i[:, None]
            masked_sorted = jnp.where(keep, vals, -jnp.inf)
            rows = jnp.arange(n)[:, None]
            masked = jnp.full_like(logits, -jnp.inf).at[rows, order].set(masked_sorted)
            return jax.nn.softmax(masked, axis=1)
        key = jax.random.key(seed)
        ks = jax.random.split(key, 12)
        X = jax.random.normal(ks[0], (N, D_IN), jnp.float32)
        S = jax.random.uniform(ks[1], (N, N), jnp.float32)
        W1 = _xavier(ks[2], (D_IN, D_ATTN))
        W3 = _xavier(ks[3], (D_IN, D_ATTN))
        W2 = _xavier(ks[4], (D_ATTN, D_ATTN))
        U1_0 = _xavier(ks[5], (D_IN, D_IN))
        U1_1 = _xavier(ks[6], (D_IN, D_IN))
        U2_0 = _xavier(ks[7], (D_IN, D_IN))
        U2_1 = _xavier(ks[8], (D_IN, D_IN))
        gamma = jnp.ones((D_IN,), jnp.float32)
        beta = jnp.zeros((D_IN,), jnp.float32)
        return {'X': X, 'S': S, 'W1': W1, 'W2': W2, 'W3': W3, 'U1_0': U1_0, 'U1_1': U1_1, 'U2_0': U2_0, 'U2_1': U2_1, 'gamma': gamma, 'beta': beta}
    _L0_gnn_all = _L0_gnn_setup()
    _L0_gnn_in = {k: v for k, v in _L0_gnn_all.items() if k in ('W1', 'W2', 'W3', 'U1_0', 'U1_1', 'U2_0', 'U2_1', 'gamma', 'beta')}
    del _L0_gnn_all
    return {'x': x, 'adj': adj, 'L0_gnn_W1': _L0_gnn_in['W1'], 'L0_gnn_W2': _L0_gnn_in['W2'], 'L0_gnn_W3': _L0_gnn_in['W3'], 'L0_gnn_U1_0': _L0_gnn_in['U1_0'], 'L0_gnn_U1_1': _L0_gnn_in['U1_1'], 'L0_gnn_U2_0': _L0_gnn_in['U2_0'], 'L0_gnn_U2_1': _L0_gnn_in['U2_1'], 'L0_gnn_gamma': _L0_gnn_in['gamma'], 'L0_gnn_beta': _L0_gnn_in['beta']}

def reference(x, adj, L0_gnn_W1, L0_gnn_W2, L0_gnn_W3, L0_gnn_U1_0, L0_gnn_U1_1, L0_gnn_U2_0, L0_gnn_U2_1, L0_gnn_gamma, L0_gnn_beta):
    import jax
    import jax.numpy as jnp

    def _L0_gnn_ref(X, S, W1, W2, W3, U1_0, U1_1, U2_0, U2_1, gamma, beta):
        import jax, jax.numpy as jnp
        import numpy as np
        D_IN, D_ATTN, STEPS = (512, 64, 2)
        P_TOP, TAU, LN_EPS = (0.9, 1.0, 1e-05)
        N = 2048

        def _xavier(key, shape):
            fan_in, fan_out = (shape[0], shape[1])
            lim = jnp.sqrt(6.0 / (fan_in + fan_out))
            return jax.random.uniform(key, shape, jnp.float32, -lim, lim)

        def _adj_from_feats(Xa, W1, W2, W3):
            Q = Xa @ W1
            K = Xa @ W3
            logits = Q @ W2 @ K.T / TAU
            n = logits.shape[1]
            order = jnp.argsort(-logits, axis=1)
            vals = jnp.take_along_axis(logits, order, axis=1)
            probs = jax.nn.softmax(vals, axis=1)
            csum = jnp.cumsum(probs, axis=1)
            k_i = jnp.sum(csum < P_TOP, axis=1) + 1
            keep = jnp.arange(n)[None, :] < k_i[:, None]
            masked_sorted = jnp.where(keep, vals, -jnp.inf)
            rows = jnp.arange(n)[:, None]
            masked = jnp.full_like(logits, -jnp.inf).at[rows, order].set(masked_sorted)
            return jax.nn.softmax(masked, axis=1)
        n = X.shape[0]
        S = S + jnp.eye(n, dtype=X.dtype)
        R = S / jnp.clip(S.sum(axis=1, keepdims=True), 1e-12)
        Z = jnp.zeros_like(X)
        Xf, Xa = (X, X)
        U1s, U2s = ((U1_0, U1_1), (U2_0, U2_1))
        for s in range(STEPS):
            A = _adj_from_feats(Xa, W1, W2, W3)
            Xf = R @ Xf
            Xa = A @ Xa
            Z = Z + (Xf @ U1s[s] + Xa @ U2s[s])
        Y = X + Z
        mu = Y.mean(axis=-1, keepdims=True)
        var = Y.var(axis=-1, keepdims=True)
        return (Y - mu) * jax.lax.rsqrt(var + LN_EPS) * gamma + beta
    h = jnp.maximum(_layernorm(x, axis=-1), 0.0)
    x = x + _L0_gnn_ref(h, adj, L0_gnn_W1, L0_gnn_W2, L0_gnn_W3, L0_gnn_U1_0, L0_gnn_U1_1, L0_gnn_U2_0, L0_gnn_U2_1, L0_gnn_gamma, L0_gnn_beta)
    return x

_drawn_inputs = setup_inputs


def setup_inputs(seed=0):
    import zlib

    import numpy as np

    out = dict(_drawn_inputs(seed))
    spreads = {'L0_gnn_gamma': (1.0, 0.2), 'L0_gnn_beta': (0.0, 0.1)}
    factors = {}
    for name, (base, spread) in spreads.items():
        noise = np.random.default_rng([zlib.crc32(name.encode()), seed]).standard_normal(out[name].shape)
        drawn = base * np.exp(spread * noise) if base else spread * noise
        out[name] = jnp.asarray(drawn.astype(out[name].dtype))
    for name, factor in factors.items():
        out[name] = (out[name] * factor).astype(out[name].dtype)
    return out
```

```python
import math


def build_top_p_gnn(nc, x, adj, W1, W2, W3, U1_0, U1_1, U2_0, U2_1, gamma, beta, out):
    import concourse.bass as bass
    from concourse import mybir
    from contextlib import ExitStack

    f32, f16, i32 = mybir.dt.float32, mybir.dt.float16, mybir.dt.int32
    ALU, ACT, AX = mybir.AluOpType, mybir.ActivationFunctionType, mybir.AxisListType

    P = 128
    N, D = x.shape
    DA = W2.shape[0]
    T = -(-N // P)
    NP = T * P
    TAIL = N - (T - 1) * P
    assert T % 2 == 0 and D == 4 * P and DA == 64
    DC = D // P
    GB = 4
    NG = -(-T // GB)
    CHUNK = 512
    NCH = -(-NP // CHUNK)
    assert NG == NCH and NG % 2 == 1
    FS, RSC = 2.0 ** 10, 2.0 ** 14
    P_TOP, EPS = 0.9, 1e-5
    PASSES = (8, 11)
    ALL_PASSES = 27
    TOP = RSC * 1.001
    BOTTOM = RSC * (1 - P_TOP) / NP * 0.95
    SPAN = math.log(TOP / BOTTOM)
    BIG = 1e30
    blocks = [range(g * GB, min(T, (g + 1) * GB)) for g in range(NG)]

    def ratio(k):
        return math.exp(SPAN / 2 ** (k + 1))

    h_plus_z = nc.dram_tensor("h_plus_z", [T, P, D], f32).ap()
    xa_next = nc.dram_tensor("xa_next", [T, P, 2 * D], f16).ap()
    q_dram = nc.dram_tensor("q_dram", [2, T, DA, P], f32).ap()
    k_dram = nc.dram_tensor("k_dram", [2, DA, NP], f32).ap()
    rt_dram = nc.dram_tensor("rt_dram", [T, P, T, 2 * P], f16).ap()

    with ExitStack() as ctx:
        def sb(name, shape, dt):
            return ctx.enter_context(nc.sbuf_tensor(name, shape, dt))

        def ps(name, shape):
            return ctx.enter_context(nc.psum_tensor(name, shape, f32))

        def sem(name):
            return ctx.enter_context(nc.semaphore(name))

        XA = sb("XA", [P, T, 2 * D], f16)
        XBf = sb("XBf", [P, T, D], f32)
        XB = XBf[:, :, :].bitcast(f16)
        KQ = sb("KQ", [P, NP], f32)
        KT = KQ[0:DA, :]
        w2, qf = KQ[DA:2 * DA, 0:P], KQ[DA:2 * DA, P:2 * P]
        U1 = sb("U1", [P, DC, D], f32)
        U2 = sb("U2", [P, DC, D], f32)
        E = [sb(f"E{i}", [P, NP], f32) for i in range(2)]
        JK = sb("JK", [P, NP], f32)
        AD = sb("AD", [P, NP], f32)
        RT = AD[:, :].bitcast(f16).rearrange("p (b c) -> p b c", c=2 * P)
        ringR = [sb(f"ringR{i}", [P, GB, 2 * P], f16) for i in range(2)]
        ringA = [sb(f"ringA{i}", [P, GB, 2 * P], f16) for i in range(2)]
        XN = [sb(f"XN{i}", [P, D], f32) for i in range(2)]
        xT = sb("xT", [P, DC, P], f32)
        zt = sb("zt", [P, D], f32)
        xah = sb("xah", [P, 2 * D], f16)
        w13 = sb("w13", [P, DC, 2 * DA], f32)
        ident = sb("ident", [P, P], f32)
        qs = [sb(f"qs{i}", [DA, P], f32) for i in range(2)]
        qk = sb("qk", [P, P], f32)
        mv = sb("mv", [P, T, 2], f32)
        stdev = sb("stdev", [P, 32], f32)
        rstd = stdev[:, 0:T]
        cols = sb("cols", [P, 64], f32)
        flag_i = sb("flag_i", [P, 1], i32)
        names = ["neg_max", "goal", "lo", "hi", "t", "mass", "mass_hi", "up", "far", "v_star", "v_more",
                 "mass_gt", "n_tie", "reach", "bad", "quota", "below", "gap", "kept", "row_sum", "row_scale",
                 "eps", "tmp", "tmp2"]
        col = {n: cols[:, i:i + 1] for i, n in enumerate(names)}
        nb = [cols[:, 24 + i:25 + i] for i in range(2)]
        S = [cols[:, 26 + i:27 + i] for i in range(2)]
        rinv = [cols[:, 28 + i:29 + i] for i in range(2)]
        v8, cum8, w8 = cols[:, 32:40], cols[:, 40:48], cols[:, 48:56]
        mx8 = cols[:, 56:56 + NCH]
        flags = sb("flags", [P, 32], f32)
        flagsT = stdev
        st6, moments = w8[:, 0:6], cols[:, 30:32]
        halving = sb("halving", [P, ALL_PASSES - min(PASSES)], f32)

        pL = [ps(f"pL{i}", [P, CHUNK]) for i in range(2)]
        pT = [ps(f"pT{i}", [P, GB, P]) for i in range(2)]
        pR, pA, pZ = ps("pR", [P, D]), ps("pA", [P, D]), ps("pZ", [P, D])
        pX = ps("pX", [P, DC, P])

        x_in, w_in, k_in, xa_in = sem("x_in"), sem("w_in"), sem("k_in"), sem("xa_in")
        q_in = [sem("q_in0"), sem("q_in1")]
        z_in, adj_in, rt_in = sem("z_in"), sem("adj_in"), sem("rt_in")
        ident_made, consts_made = sem("ident_made"), sem("consts_made")
        stats_made, root_made = sem("stats_made"), sem("root_made")
        h_made, h_hi = sem("h_made"), sem("h_hi")
        h_stored = [sem("h_stored0"), sem("h_stored1")]
        logits_made, logits_taken = sem("logits_made"), sem("logits_taken")
        max_made, exp_made, mask_made = sem("max_made"), sem("exp_made"), sem("mask_made")
        R_turned, R_hi, R_lo, R_used = sem("R_turned"), sem("R_hi"), sem("R_lo"), sem("R_used")
        A_turned, A_hi, A_lo, A_used = sem("A_turned"), sem("A_hi"), sem("A_lo"), sem("A_used")
        R_stored = [sem("R_stored0"), sem("R_stored1")]
        adj_eye, adj_summed, adj_recip, adj_scaled = sem("adj_eye"), sem("adj_summed"), sem("adj_recip"), sem("adj_scaled")
        xnR_made, xnA_made = sem("xnR_made"), sem("xnA_made")
        lo_made = sem("lo_made")
        x_turned, xT_made = sem("x_turned"), sem("xT_made")
        z_added, z_taken = sem("z_added"), sem("z_taken")
        qk_made, qf_made, q2_made, q2_taken = sem("qk_made"), sem("qf_made"), sem("q2_made"), sem("q2_taken")
        z_stored, xa_stored, qk_stored = sem("z_stored"), sem("xa_stored"), sem("qk_stored")
        gb_made, gb_taken, ones_made = sem("gb_made"), sem("gb_taken"), sem("ones_made")
        y_in = [sem("y_in0"), sem("y_in1")]
        y_scaled, y_done = sem("y_scaled"), sem("y_done")
        out_stored = [sem("out_stored0"), sem("out_stored1")]

        block = ctx.enter_context(nc.Block())

        def tiles(engine, body):
            with engine.Fori(0, T // 2 - 1) as j:
                body(j * 2, j, 0, False)
                body(j * 2 + 1, j, 1, False)
            body(T - 2, T // 2 - 1, 0, False)
            body(T - 1, T // 2 - 1, 1, True)

        def following(i, j, par):
            return i + 1, j + par, 1 - par

        @block.sync
        def _(sp):
            full = (T - 1) * P
            sp.wait_ge(consts_made, 1)
            sp.dma_start(XBf[:, 0:T - 1, :], x[0:full, :].rearrange("(t p) d -> p t d", p=P)).then_inc(x_in, 16)
            sp.dma_start(XBf[0:TAIL, T - 1, :], x[full:N, :]).then_inc(x_in, 16)
            sp.dma_start(w13[:, :, 0:DA], W1.rearrange("(c p) a -> p c a", p=P)).then_inc(w_in, 16)
            sp.dma_start(w13[:, :, DA:2 * DA], W3.rearrange("(c p) a -> p c a", p=P)).then_inc(w_in, 16)
            sp.dma_start(w2[:, 0:DA], W2).then_inc(w_in, 16)
            sp.dma_start(U1[:, :, :], U1_0.rearrange("(c p) a -> p c a", p=P)).then_inc(w_in, 16)
            sp.dma_start(U2[:, :, :], U2_0.rearrange("(c p) a -> p c a", p=P)).then_inc(w_in, 16)
            sp.dma_start(AD[:, 0:N], adj[0:P, :]).then_inc(adj_in, 16)

            def store_qk(s, i, n):
                sp.wait_ge(q2_taken, n + 1)
                sp.dma_start(q_dram[s, bass.ds(i, 1), :, :].rearrange("o a c -> (o a) c"), qk[0:DA, :]).then_inc(qk_stored, 16)
                sp.dma_start(k_dram[s, :, bass.ds(i * P, P)], qk[DA:2 * DA, :]).then_inc(qk_stored, 16)

            def phase0(i, j, par):
                sp.wait_ge(h_made, i + 1)
                sp.dma_start(h_plus_z[bass.ds(i, 1), :, :].rearrange("o p d -> (o p) d"), XN[par][:, :]).then_inc(h_stored[par], 16)
                store_qk(0, i, i)

            with sp.Fori(0, T // 2) as j:
                phase0(j * 2, j, 0)
                phase0(j * 2 + 1, j, 1)
            for par in range(2):
                sp.wait_ge(h_stored[par], 16 * (T // 2))

            def load_q(s, i, par):
                sp.dma_start(qs[par][:, :], q_dram[s, bass.ds(i, 1), :, :].rearrange("o a c -> (o a) c")).then_inc(q_in[par], 16)

            def tile(s, i, j, par, last, last_pair):
                g = s * T + i
                if not last_pair:
                    sp.wait_ge(logits_made, (g + 1) * NCH)
                    load_q(s, i + 2, par)
                sp.wait_ge(z_stored, 16 * (g + 1))
                sp.dma_start(zt[:, :], h_plus_z[bass.ds(i, 1), :, :].rearrange("o p d -> (o p) d")).then_inc(z_in, 16)
                if s == 0:
                    for k, bl in enumerate(blocks):
                        slot = (par * NG + k) % 2
                        sp.wait_ge(R_lo, g * NG + k + 1)
                        sp.dma_start(rt_dram[bass.ds(i, 1), :, bl[0]:bl[-1] + 1, :].rearrange("o p b c -> (o p) b c"),
                                     ringR[slot][:, 0:len(bl), :]).then_inc(R_stored[slot], 16)
                    if not last:
                        sp.wait_ge(R_turned, (g + 1) * NG)
                        if last_pair:
                            sp.dma_start(AD[0:TAIL, 0:N], adj[full:N, :]).then_inc(adj_in, 16)
                        else:
                            sp.dma_start(AD[:, 0:N], adj[bass.ds((i + 1) * P, P), :]).then_inc(adj_in, 16)
                    sp.wait_ge(xnA_made, g + 2)
                    sp.wait_ge(lo_made, T + 2 * (i + 1))
                    sp.dma_start(xa_next[bass.ds(i, 1), :, :].rearrange("o p d -> (o p) d"), xah[:, :]).then_inc(xa_stored, 16)
                    store_qk(1, i, T + i)
                elif not last:
                    sp.wait_ge(R_used, (g + 1) * NG + 2)
                    sp.dma_start(RT, rt_dram[bass.ds(i + 1, 1), :, :, :].rearrange("o p b c -> (o p) b c")).then_inc(rt_in, 16)
                sp.wait_ge(z_taken, g + 2)
                sp.dma_start(h_plus_z[bass.ds(i, 1), :, :].rearrange("o p d -> (o p) d"), zt[:, :]).then_inc(z_stored, 16)

            for s in range(2):
                sp.wait_ge(qk_stored, 32 + 32 * T * (s + 1))
                if s == 1:
                    sp.wait_ge(xa_stored, 16 * (T + 1))
                    sp.wait_ge(A_used, T * NG + 2)
                    sp.wait_ge(R_used, T * NG + 2)
                    sp.wait_ge(z_added, 2 * T)
                    sp.wait_ge(z_stored, 16 * (T + 1))
                    for par in range(2):
                        n = T * NG // 2
                        sp.wait_ge(R_stored[par], 16 * (n + 1))
                sp.dma_start(KT, k_dram[s, :, :]).then_inc(k_in, 16)
                for par in range(2):
                    load_q(s, par, par)
                if s == 1:
                    sp.dma_start(RT, rt_dram[0, :, :, :]).then_inc(rt_in, 16)
                    for half in range(2):
                        a, b = half * T // 2, (half + 1) * T // 2
                        sp.dma_start(XA[:, a:b, :], xa_next[a:b, :, :].rearrange("t p d -> p t d")).then_inc(xa_in, 16)
                    sp.dma_start(U1[:, :, :], U1_1.rearrange("(c p) a -> p c a", p=P)).then_inc(w_in, 16)
                    sp.dma_start(U2[:, :, :], U2_1.rearrange("(c p) a -> p c a", p=P)).then_inc(w_in, 16)
                with sp.Fori(0, T // 2 - 1) as j:
                    tile(s, j * 2, j, 0, False, False)
                    tile(s, j * 2 + 1, j, 1, False, False)
                tile(s, T - 2, T // 2 - 1, 0, False, True)
                tile(s, T - 1, T // 2 - 1, 1, True, True)

            sp.wait_ge(z_stored, 16 * (2 * T + 1))
            sp.wait_ge(mask_made, 2 * T)
            sp.wait_ge(A_used, 2 * T * NG + 2)
            sp.wait_ge(z_added, 4 * T)
            sp.dma_start(U1[0:1, 0, :], gamma.rearrange("(o d) -> o d", o=1)).then_inc(w_in, 16)
            sp.dma_start(U1[0:1, 1, :], beta.rearrange("(o d) -> o d", o=1)).then_inc(w_in, 16)

            def last_phase(i, j, par, rows, x_rows):
                sp.wait_ge(out_stored[par], 16 * (j + 1))
                sp.dma_start(E[par][:, 0:D], h_plus_z[bass.ds(i, 1), :, :].rearrange("o p d -> (o p) d")).then_inc(y_in[par], 16)
                sp.dma_start(E[par][0:rows, D:2 * D], x_rows).then_inc(y_in[par], 16)

            def last_store(i, par, rows, out_rows):
                sp.wait_ge(y_done, i + 1)
                sp.dma_start(out_rows, E[par][0:rows, 0:D]).then_inc(out_stored[par], 16)

            with sp.Fori(0, T // 2 - 1) as j:
                for par in range(2):
                    i = j * 2 + par
                    last_phase(i, j, par, P, x[bass.ds(i * P, P), :])
                for par in range(2):
                    i = j * 2 + par
                    last_store(i, par, P, out[bass.ds(i * P, P), :])
            j = T // 2 - 1
            last_phase(T - 2, j, 0, P, x[(T - 2) * P:(T - 1) * P, :])
            last_phase(T - 1, j, 1, TAIL, x[full:N, :])
            last_store(T - 2, 0, P, out[(T - 2) * P:(T - 1) * P, :])
            last_store(T - 1, 1, TAIL, out[full:N, :])
            for par in range(2):
                sp.wait_ge(out_stored[par], 16 * (T // 2 + 1))

        @block.gpsimd
        def _(pool):
            nc.gpsimd.memset(ident[:, :], 0.0).then_inc(ident_made, 1)
            pool.wait_ge(ident_made, 1)
            nc.gpsimd.affine_select(out=ident[:, :], in_=ident[:, :], compare_op=ALU.not_equal, fill=1.0, base=0,
                                    pattern=[[-1, P]], channel_multiplier=1).then_inc(ident_made, 1)
            pool.wait_ge(ident_made, 2)

            def phase0(i, par):
                pool.wait_ge(h_made, i + 1)
                pool.wait_ge(h_hi, i + 1)
                nc.gpsimd.tensor_tensor(XA[:, bass.ds(i, 1), D:2 * D].rearrange("p o d -> p (o d)"), XN[par][:, :],
                                        XA[:, bass.ds(i, 1), 0:D].rearrange("p o d -> p (o d)"),
                                        ALU.subtract).then_inc(lo_made, 1)

            with pool.Fori(0, T // 2) as j:
                phase0(j * 2, 0)
                phase0(j * 2 + 1, 1)

            def add_eye(i):
                pool.wait_ge(adj_in, 16 * (i + 1))
                blk = AD[:, bass.ds(i * P, P)]
                nc.gpsimd.tensor_tensor(blk, blk, ident[:, :], ALU.add).then_inc(adj_eye, 1)

            add_eye(0)

            def tile0(i, j, par, last):
                if not last:
                    add_eye(i + 1)
                pool.wait_ge(xnR_made, i + 2)
                nc.gpsimd.tensor_tensor(XB[:, bass.ds(i, 1), D:2 * D].rearrange("p o d -> p (o d)"), XN[0][:, :],
                                        XB[:, bass.ds(i, 1), 0:D].rearrange("p o d -> p (o d)"),
                                        ALU.subtract).then_inc(lo_made, 1)
                pool.wait_ge(xnA_made, i + 2)
                nc.gpsimd.tensor_tensor(xah[:, D:2 * D], XN[1][:, :], xah[:, 0:D], ALU.subtract).then_inc(lo_made, 1)

            tiles(pool, tile0)

            def last_phase(i, j, par):
                pool.wait_ge(y_scaled, i + 1)
                pool.wait_ge(gb_taken, 2)
                y, xx = E[par][:, 0:D], E[par][:, D:2 * D]
                nc.gpsimd.tensor_tensor(xx, xx, U1[:, 3, :], ALU.add)
                pool.drain()
                nc.gpsimd.tensor_tensor(y, y, xx, ALU.add).then_inc(y_done, 1)

            with pool.Fori(0, T // 2) as j:
                last_phase(j * 2, j, 0)
                last_phase(j * 2 + 1, j, 1)

        @block.scalar
        def _(act):
            act.wait_ge(stats_made, 1)
            nc.scalar.activation(rstd[:, :], mv[:, :, 1], ACT.Sqrt, bias=col["eps"]).then_inc(root_made, 1)

            def take_xT(n):
                act.wait_ge(x_turned, n + 1)
                nc.scalar.activation(xT[:, :, :], pX[:, :, :], ACT.Copy).then_inc(xT_made, 1)

            def take_qk(n):
                act.wait_ge(qk_made, n + 1)
                act.wait_ge(qk_stored, 32 * (n + 1))
                nc.scalar.activation(qf, pX[0:DA, 0, :], ACT.Copy)
                nc.scalar.activation(qk[DA:2 * DA, :], pX[DA:2 * DA, 0, :], ACT.Copy).then_inc(qf_made, 1)
                act.wait_ge(q2_made, n + 1)
                nc.scalar.activation(qk[0:DA, :], pX[0:DA, 1, :], ACT.Copy).then_inc(q2_taken, 1)

            def phase0(i, par):
                act.wait_ge(h_made, i + 1)
                nc.scalar.activation(XA[:, bass.ds(i, 1), 0:D].rearrange("p o d -> p (o d)"), XN[par][:, :], ACT.Copy).then_inc(h_hi, 1)
                take_xT(i)
                take_qk(i)

            with act.Fori(0, T // 2) as j:
                phase0(j * 2, 0)
                phase0(j * 2 + 1, 1)

            def exp(s, i, par):
                act.wait_ge(max_made, s * T + i + 1)
                nc.scalar.activation(E[par][:, 0:N], E[par][:, 0:N], ACT.Exp, bias=nb[par], scale=1.0 / FS ** 2,
                                     accum_out=S[par]).then_inc(exp_made, 1)

            def adj_sum(i):
                act.wait_ge(adj_eye, i + 1)
                nc.scalar.activation(AD[:, :], AD[:, :], ACT.Copy, accum_out=col["row_sum"]).then_inc(adj_summed, 1)

            def adj_scale(i):
                act.wait_ge(adj_recip, i + 1)
                nc.scalar.activation(AD[:, :], AD[:, :], ACT.Copy, scale=col["row_scale"]).then_inc(adj_scaled, 1)

            def hi_part(turned, used, made, ring, s, g, par, k, bank):
                n = g * NG + k
                slot = (par * NG + k) % 2
                act.wait_ge(turned, n + 2)
                act.wait_ge(used, n + 1)
                m = len(blocks[k])
                nc.scalar.activation(ring[slot][:, 0:m, 0:P], pT[bank][:, 0:m, :], ACT.Copy).then_inc(made, 1)

            def tile(s, i, j, par, last):
                g = s * T + i
                if not last:
                    exp(s, i + 1, 1 - par)
                if s == 0:
                    for k in range(NG):
                        slot = (par * NG + k) % 2
                        act.wait_ge(R_stored[slot], 16 * (j * NG + (par * NG + k) // 2 + 1))
                        n = g * NG + k
                        act.wait_ge(R_turned, n + 1)
                        act.wait_ge(R_used, n + 1)
                        m = len(blocks[k])
                        nc.scalar.activation(ringR[slot][:, 0:m, 0:P], pT[k % 2][:, 0:m, :], ACT.Copy).then_inc(R_hi, 1)
                for k in range(NG):
                    bank = (k + 1) % 2 if s == 0 else (par * NG + k) % 2
                    hi_part(A_turned, A_used, A_hi, ringA, s, g, par, k, bank)
                    if s == 0 and not last and k == min(2, NG - 1):
                        adj_sum(i + 1)
                    if s == 0 and not last and k == min(4, NG - 1):
                        adj_scale(i + 1)
                act.wait_ge(R_used, (g + 1) * NG + 2)
                act.wait_ge(x_turned, T + 2 * g)
                if s == 0:
                    act.wait_ge(lo_made, T + 2 * i)
                    nc.scalar.activation(XB[:, bass.ds(i, 1), 0:D].rearrange("p o d -> p (o d)"), pR[:, :], ACT.Copy,
                                         scale=1.0 / RSC)
                nc.scalar.activation(XN[0][:, :], pR[:, :], ACT.Copy, scale=1.0 / RSC).then_inc(xnR_made, 1)
                act.wait_ge(A_used, (g + 1) * NG + 2)
                if s == 0:
                    act.wait_ge(xa_stored, 16 * (i + 1))
                    nc.scalar.activation(xah[:, 0:D], pA[:, :], ACT.Copy, scale=rinv[par])
                nc.scalar.activation(XN[1][:, :], pA[:, :], ACT.Copy, scale=rinv[par]).then_inc(xnA_made, 1)
                if s == 0:
                    act.wait_ge(qk_made, T + i)
                else:
                    act.wait_ge(z_added, 2 * g)
                take_xT(T + 2 * g)
                act.wait_ge(z_added, 2 * g + 1)
                take_xT(T + 2 * g + 1)
                if s == 0:
                    take_qk(T + i)

            adj_sum(0)
            adj_scale(0)
            for s in range(2):
                exp(s, 0, 0)
                tiles(act, lambda i, j, par, last: tile(s, i, j, par, last))

            act.wait_ge(stats_made, 2)
            nc.scalar.activation(rstd[:, :], mv[:, :, 1], ACT.Sqrt, bias=col["eps"]).then_inc(root_made, 1)
            act.wait_ge(gb_made, 2)
            nc.scalar.activation(U1[:, 2, :], pR[:, :], ACT.Copy).then_inc(gb_taken, 1)
            nc.scalar.activation(U1[:, 3, :], pA[:, :], ACT.Copy).then_inc(gb_taken, 1)

        @block.vector
        def _(dve):
            nc.vector.memset(XBf[:, T - 1, :], 0.0).then_inc(consts_made, 1)
            for k in range(ALL_PASSES - min(PASSES)):
                nc.vector.memset(halving[:, k:k + 1], ratio(min(PASSES) + k))
            nc.vector.memset(flags[:, :], 0.0)
            nc.vector.memset(w2[:, DA:P], 0.0)
            nc.vector.memset(col["eps"], EPS)
            nc.vector.memset(E[0][:, N:NP], 0.0)
            nc.vector.memset(E[1][:, N:NP], 0.0)
            nc.vector.memset(AD[:, N:NP], 0.0)
            dve.drain()
            for free, n in ((logits_taken, 2), (A_turned, 1), (A_lo, 2), (R_used, 2), (A_used, 2), (R_stored[0], 16),
                            (R_stored[1], 16), (xnR_made, 1), (xnA_made, 1), (z_taken, 1), (z_stored, 16),
                            (xa_stored, 16), (qk_stored, 32), (out_stored[0], 16), (out_stored[1], 16)):
                dve.sem_inc(free, n)

            dve.wait_ge(x_in, 32)

            def stats(i, src):
                nc.vector.bn_stats(st6, src)
                dve.drain()
                nc.vector.bn_aggr(moments, st6)
                dve.drain()
                nc.vector.tensor_copy(mv[:, bass.ds(i, 1), :].rearrange("p o c -> p (o c)"), moments)

            with dve.Fori(0, T) as i:
                stats(i, XBf[:, bass.ds(i, 1), :].rearrange("p o d -> p (o d)"))
            dve.drain().then_inc(stats_made, 1)
            dve.wait_ge(root_made, 1)
            nc.vector.reciprocal(rstd[:, :], rstd[:, :])
            dve.drain()

            def phase0(i, j, par, first):
                xi = XBf[:, bass.ds(i, 1), :].rearrange("p o d -> p (o d)")
                nc.vector.tensor_scalar(xi, xi, mv[:, bass.ds(i, 1), 0], rstd[:, bass.ds(i, 1)], ALU.subtract, ALU.mult)
                dve.drain()
                if not first:
                    dve.wait_ge(x_turned, i - 1)
                    dve.wait_ge(h_hi, i - 1)
                    dve.wait_ge(lo_made, i - 1)
                    dve.wait_ge(h_stored[par], 16 * j)
                nc.vector.tensor_scalar(XN[par][:, :], xi, 0.0, FS, ALU.max, ALU.mult).then_inc(h_made, 1)

            phase0(0, 0, 0, True)
            phase0(1, 0, 1, True)
            with dve.Fori(1, T // 2) as j:
                phase0(j * 2, j, 0, False)
                phase0(j * 2 + 1, j, 1, False)

            def take_logits(s, i, par):
                g = s * T + i
                if not isinstance(i, int) or i >= 2 or s == 1:
                    dve.wait_ge(A_turned, (g - 1) * NG + 1)
                for c in range(NCH):
                    w = min(CHUNK, N - c * CHUNK)
                    dve.wait_ge(logits_made, g * NCH + c + 1)
                    nc.vector.tensor_scalar(E[par][:, c * CHUNK:c * CHUNK + w], pL[(par + c) % 2][:, 0:w], 1.0, None,
                                            ALU.mult, ALU.max, accum_out=mx8[:, c:c + 1]).then_inc(logits_taken, 1)
                dve.drain()
                nc.vector.tensor_reduce(col["neg_max"], mx8, AX.X, ALU.max)
                dve.drain()
                nc.vector.tensor_scalar(nb[par], col["neg_max"], -1.0 / FS ** 2, math.log(RSC), ALU.mult, ALU.add).then_inc(max_made, 1)

            def lo_parts(turned_hi, made, ring, g, par, k, bank):
                slot, m = (par * NG + k) % 2, len(blocks[k])
                dve.wait_ge(turned_hi, g * NG + k + 1)
                nc.vector.tensor_tensor(ring[slot][:, 0:m, P:2 * P], pT[bank][:, 0:m, :], ring[slot][:, 0:m, 0:P],
                                        ALU.subtract).then_inc(made, 1)

            def mass_pass(par):
                c = col
                nc.vector.scalar_tensor_tensor(out=JK[:, 0:N], in0=E[par][:, 0:N], scalar=c["t"], in1=E[par][:, 0:N],
                                               op0=ALU.is_gt, op1=ALU.mult, accum_out=c["mass"])
                dve.drain()
                nc.vector.tensor_scalar(c["up"], c["mass"], c["goal"], None, ALU.is_ge)
                dve.drain()
                nc.vector.scalar_tensor_tensor(out=c["lo"], in0=c["up"], scalar=c["t"], in1=c["lo"], op0=ALU.mult, op1=ALU.max)
                nc.vector.scalar_tensor_tensor(out=c["far"], in0=c["up"], scalar=BIG, in1=c["t"], op0=ALU.mult, op1=ALU.add)
                nc.vector.scalar_tensor_tensor(out=c["tmp"], in0=c["up"], scalar=-BIG, in1=c["mass"], op0=ALU.mult, op1=ALU.add)
                dve.drain()
                nc.vector.tensor_tensor(c["hi"], c["hi"], c["far"], ALU.min)
                nc.vector.tensor_tensor(c["mass_hi"], c["mass_hi"], c["tmp"], ALU.max)

            def threshold(par):
                c = col
                e, jk = E[par][:, 0:N], JK[:, 0:N]
                nc.vector.scalar_tensor_tensor(out=jk, in0=e, scalar=c["hi"], in1=e, op0=ALU.is_le, op1=ALU.mult)
                dve.drain()
                nc.vector.max(v8, jk)
                dve.drain()
                nc.vector.tensor_tensor_scan(cum8, v8, v8, c["mass_hi"], ALU.add, ALU.max)
                dve.drain()
                nc.vector.scalar_tensor_tensor(out=w8, in0=cum8, scalar=c["goal"], in1=v8, op0=ALU.is_ge, op1=ALU.mult)
                dve.drain()
                nc.vector.tensor_reduce(c["tmp"], w8, AX.X, ALU.max)
                dve.drain()
                nc.vector.tensor_tensor(c["v_star"], c["tmp"], v8[:, 7:8], ALU.max)
                dve.drain()
                nc.vector.scalar_tensor_tensor(out=w8, in0=v8, scalar=c["v_star"], in1=v8, op0=ALU.is_gt, op1=ALU.mult,
                                               accum_out=c["v_more"])
                nc.vector.tensor_scalar(jk, e, c["v_star"], None, ALU.is_equal)
                dve.drain()
                nc.vector.tensor_tensor(c["mass_gt"], c["mass_hi"], c["v_more"], ALU.add)
                nc.vector.tensor_tensor_scan(jk, jk, jk, 0.0, ALU.add, ALU.max)
                dve.drain()
                nc.vector.scalar_tensor_tensor(out=c["reach"], in0=JK[:, N - 1:N], scalar=c["v_star"], in1=c["mass_gt"],
                                               op0=ALU.mult, op1=ALU.add)
                dve.drain()
                nc.vector.tensor_scalar(c["tmp"], c["reach"], c["goal"], None, ALU.is_lt)
                nc.vector.tensor_scalar(c["tmp2"], c["mass_gt"], c["goal"], None, ALU.is_ge)
                dve.drain()
                nc.vector.tensor_tensor(flags[:, 0:1], c["tmp"], c["tmp2"], ALU.max)
                dve.drain()

            def search(s, i, par, between):
                c = col
                e = E[par][:, 0:N]
                nc.vector.memset(c["lo"], BOTTOM)
                nc.vector.memset(c["hi"], TOP)
                nc.vector.memset(c["mass_hi"], 0.0)
                nc.vector.memset(c["t"], BOTTOM * ratio(0))
                dve.wait_ge(exp_made, s * T + i + 1)
                nc.vector.tensor_scalar(c["goal"], S[par], P_TOP, None, ALU.mult)
                dve.drain()
                for k in range(PASSES[s]):
                    mass_pass(par)
                    nc.vector.tensor_scalar(c["t"], c["lo"], ratio(k + 1), None, ALU.mult)
                    dve.drain()
                    between(k)
                threshold(par)
                nc.vector.transpose(flagsT[:, :], flags[:, :])
                dve.drain()
                nc.vector.tensor_reduce(c["bad"], flagsT[:, :], AX.X, ALU.max)
                dve.drain()
                for q in range(4):
                    nc.vector.tensor_copy(w8[0:1, q:q + 1], c["bad"][32 * q:32 * q + 1, :])
                dve.drain()
                nc.vector.tensor_reduce(c["tmp"][0:1, :], w8[0:1, 0:4], AX.X, ALU.max)
                dve.drain()
                nc.vector.tensor_copy(flag_i[0:1, :], c["tmp"][0:1, :])
                dve.drain()
                unsettled = dve.value_load(flag_i[0:1, 0:1], min_val=0, max_val=1)
                with dve.If(unsettled != 0):
                    with dve.Fori(PASSES[s] - min(PASSES), ALL_PASSES - min(PASSES)) as k:
                        nc.vector.tensor_tensor(c["t"], c["lo"], halving[:, bass.ds(k, 1)], ALU.mult)
                        dve.drain()
                        mass_pass(par)
                        dve.drain()
                    threshold(par)
                with dve.Else():
                    dve.drain()
                nc.vector.tensor_tensor(c["tmp"], c["goal"], c["mass_gt"], ALU.subtract)
                nc.vector.reciprocal(c["tmp2"], c["v_star"])
                nc.vector.tensor_scalar(c["below"], c["v_star"], 1.0 - 2.0 ** -24, None, ALU.mult)
                dve.drain()
                nc.vector.tensor_scalar(c["quota"], c["tmp"], c["tmp2"], 1.0, ALU.mult, ALU.add)
                nc.vector.tensor_tensor(c["gap"], c["v_star"], c["below"], ALU.subtract)
                dve.drain()
                jk = JK[:, 0:N]
                nc.vector.tensor_scalar(jk, jk, c["quota"], c["gap"], ALU.is_ge, ALU.mult)
                dve.drain()
                nc.vector.scalar_tensor_tensor(out=jk, in0=jk, scalar=c["below"], in1=e, op0=ALU.add, op1=ALU.is_lt)
                dve.drain()
                nc.vector.scalar_tensor_tensor(out=e, in0=jk, scalar=1.0, in1=e, op0=ALU.mult, op1=ALU.mult,
                                               accum_out=c["kept"])
                dve.drain()
                nc.vector.reciprocal(rinv[par], c["kept"]).then_inc(mask_made, 1)

            def adj_recip_of(i):
                dve.wait_ge(adj_summed, i + 1)
                nc.vector.tensor_scalar(col["row_sum"], col["row_sum"], 1e-12, 1.0 / RSC, ALU.max, ALU.mult)
                dve.drain()
                nc.vector.reciprocal(col["row_scale"], col["row_sum"]).then_inc(adj_recip, 1)

            def tile(s, i, par, last):
                g = s * T + i
                if not last:
                    take_logits(s, i + 1, 1 - par)
                if s == 0:
                    for k in range(NG):
                        lo_parts(R_hi, R_lo, ringR, g, par, k, k % 2)

                def between(k):
                    if k < NG:
                        lo_parts(A_hi, A_lo, ringA, g, par, k, (k + 1) % 2 if s == 0 else (par * NG + k) % 2)
                        if k == min(3, NG - 1) and s == 0 and not last:
                            adj_recip_of(i + 1)

                if last:
                    for k in range(NG):
                        between(k)
                else:
                    search(s, i + 1, 1 - par, between)
                dve.wait_ge(z_in, 16 * (g + 1))
                dve.wait_ge(z_added, 2 * (g + 1))
                nc.vector.tensor_tensor(zt[:, :], pZ[:, :], zt[:, :], ALU.add)
                dve.drain()
                if s == 1:
                    stats(i, zt[:, :])
                dve.drain().then_inc(z_taken, 1)

            adj_recip_of(0)
            for s in range(2):
                take_logits(s, 0, 0)
                search(s, 0, 0, lambda k: None)
                tiles(dve, lambda i, j, par, last: tile(s, i, par, last))

            nc.vector.memset(col["eps"], EPS * FS ** 2)
            nc.vector.memset(qs[0][0:1, :], 1.0).then_inc(ones_made, 1)
            dve.drain().then_inc(stats_made, 1)
            dve.wait_ge(root_made, 2)
            nc.vector.reciprocal(rstd[:, :], rstd[:, :])
            dve.drain()
            dve.wait_ge(gb_taken, 2)

            def last_phase(i, j, par):
                y = E[par][:, 0:D]
                dve.wait_ge(y_in[par], 32 * (j + 1))
                nc.vector.tensor_scalar(y, y, mv[:, bass.ds(i, 1), 0], rstd[:, bass.ds(i, 1)], ALU.subtract, ALU.mult)
                dve.drain()
                nc.vector.tensor_tensor(y, y, U1[:, 2, :], ALU.mult).then_inc(y_scaled, 1)

            with dve.Fori(0, T // 2) as j:
                last_phase(j * 2, j, 0)
                last_phase(j * 2 + 1, j, 1)

        @block.tensor
        def _(pe):
            pe.wait_ge(ident_made, 2)
            pe.wait_ge(w_in, 16 * 5)

            def turn_x(rows, n):
                for c in range(DC):
                    last = nc.tensor.transpose(pX[:, c, :], rows[:, c * P:(c + 1) * P], ident[:, :])
                last.then_inc(x_turned, 1)
                pe.wait_ge(xT_made, n + 1)

            def query_key(n):
                for c in range(DC):
                    last = nc.tensor.matmul(pX[:, 0, :], w13[:, c, :], xT[:, c, :], start=(c == 0), stop=(c == DC - 1))
                last.then_inc(qk_made, 1)
                pe.wait_ge(qf_made, n + 1)
                nc.tensor.matmul(pX[:, 1, :], w2, qf, start=True, stop=True).then_inc(q2_made, 1)
                pe.wait_ge(q2_taken, n + 1)

            def phase0(i, par):
                pe.wait_ge(h_made, i + 1)
                turn_x(XN[par], i)
                query_key(i)

            with pe.Fori(0, T // 2) as j:
                phase0(j * 2, 0)
                phase0(j * 2 + 1, 1)

            def logits(s, i, j, par):
                g = s * T + i
                pe.wait_ge(q_in[par], 16 * (s * (T // 2) + j + 1))
                for c in range(NCH):
                    w = min(CHUNK, NP - c * CHUNK)
                    pe.wait_ge(logits_taken, g * NCH + c + 1)
                    nc.tensor.matmul(pL[(par + c) % 2][:, 0:w], qs[par][:, :], KT[:, c * CHUNK:c * CHUNK + w],
                                     start=True, stop=True).then_inc(logits_made, 1)

            def turn(src, bank, k, turned):
                for b in blocks[k]:
                    last = nc.tensor.transpose(pT[bank][:, b % GB, :], src[:, b * P:(b + 1) * P], ident[:, :])
                last.then_inc(turned, 1)

            def products(acc, weights, X, k, used):
                for b in blocks[k]:
                    whi, wlo = weights(b)
                    xhi, xlo = X[:, b, 0:D], X[:, b, D:2 * D]
                    nc.tensor.matmul(acc[:, :], whi, xhi, start=(b == 0), stop=False)
                    nc.tensor.matmul(acc[:, :], whi, xlo, start=False, stop=False)
                    last = nc.tensor.matmul(acc[:, :], wlo, xhi, start=False, stop=(b == T - 1))
                last.then_inc(used, 1)

            def ring_of(ring, par, k):
                slot = (par * NG + k) % 2
                return lambda b: (ring[slot][:, b % GB, 0:P], ring[slot][:, b % GB, P:2 * P])

            def tile(s, i, j, par, last):
                g = s * T + i
                n = g * NG
                if not last:
                    i1, j1, par1 = following(i, j, par)
                    logits(s, i1, j1, par1)
                X_R = XA if s == 0 else XB
                if s == 0:
                    pe.wait_ge(adj_scaled, i + 1)
                    for k in range(NG + 1):
                        if k < NG:
                            if k < 2:
                                pe.wait_ge(A_lo, n + k + 1)
                            else:
                                pe.wait_ge(R_lo, n + k - 1)
                            turn(AD, k % 2, k, R_turned)
                        if k == 1:
                            pe.wait_ge(xnR_made, g + 1)
                        if k >= 1:
                            pe.wait_ge(R_lo, n + k)
                            products(pR, ring_of(ringR, par, k - 1), X_R, k - 1, R_used)
                else:
                    pe.wait_ge(rt_in, 16 * (i + 1))
                    pe.wait_ge(xnR_made, g + 1)
                    for k in range(NG):
                        products(pR, lambda b: (RT[:, b, 0:P], RT[:, b, P:2 * P]), X_R, k, R_used)
                pe.wait_ge(mask_made, g + 1)
                for k in range(NG + 1):
                    if k < NG:
                        if s == 0 and k < 2:
                            pe.wait_ge(R_lo, n + NG - 1 + k)
                        else:
                            pe.wait_ge(A_lo, n + k + 1)
                        turn(E[par], (k + 1) % 2 if s == 0 else (par * NG + k) % 2, k, A_turned)
                    if k == 1:
                        pe.wait_ge(xnA_made, g + 1)
                    if k >= 1:
                        pe.wait_ge(A_lo, n + k + 2)
                        products(pA, ring_of(ringA, par, k - 1), XA, k - 1, A_used)
                pe.wait_ge(xnR_made, g + 2)
                turn_x(XN[0], T + 2 * g)
                pe.wait_ge(z_taken, g + 1)
                for c in range(DC):
                    last_z = nc.tensor.matmul(pZ[:, :], xT[:, c, :], U1[:, c, :], start=(c == 0), stop=False)
                last_z.then_inc(z_added, 1)
                pe.wait_ge(xnA_made, g + 2)
                turn_x(XN[1], T + 2 * g + 1)
                for c in range(DC):
                    last_z = nc.tensor.matmul(pZ[:, :], xT[:, c, :], U2[:, c, :], start=False, stop=(c == DC - 1))
                last_z.then_inc(z_added, 1)
                if s == 0:
                    query_key(T + i)

            for s in range(2):
                pe.wait_ge(k_in, 16 * (s + 1))
                if s == 1:
                    pe.wait_ge(xa_in, 32)
                    pe.wait_ge(w_in, 16 * 7)
                    pe.wait_ge(lo_made, 3 * T)
                logits(s, 0, 0, 0)
                tiles(pe, lambda i, j, par, last: tile(s, i, j, par, last))

            pe.wait_ge(w_in, 16 * 9)
            pe.wait_ge(ones_made, 1)
            for k, acc in ((0, pR), (1, pA)):
                nc.tensor.matmul(acc[:, :], qs[0][0:1, :], U1[0:1, k, :], start=True, stop=True).then_inc(gb_made, 1)


_INS = ["x", "adj", "L0_gnn_W1", "L0_gnn_W2", "L0_gnn_W3", "L0_gnn_U1_0", "L0_gnn_U1_1", "L0_gnn_U2_0", "L0_gnn_U2_1",
        "L0_gnn_gamma", "L0_gnn_beta"]


def kernel(**inputs):
    import numpy as _np
    import concourse.bacc as _bacc
    from concourse import mybir as _mybir
    from concourse.bass_utils import run_bass_kernel_spmd as _run

    nc = _bacc.Bacc("TRN2", target_bir_lowering=False, num_devices=1)
    arrays, args = {}, []
    for name in _INS:
        a = _np.ascontiguousarray(inputs[name])
        arrays[f"in_{name}_dram"] = a
        args.append(nc.dram_tensor(f"in_{name}_dram", a.shape, _mybir.dt.from_np(a.dtype), kind="ExternalInput").ap())
    shape = inputs["x"].shape
    args.append(nc.dram_tensor("out_dram", shape, _mybir.dt.float32, kind="ExternalOutput").ap())
    build_top_p_gnn(nc, *args)
    r = _run(nc, [arrays], core_ids=[0])
    return r.results[0]["out_dram"]
```

```python
import math


def build_top_p_gnn(nc, x, adj, W1, W2, W3, U1_0, U1_1, U2_0, U2_1, gamma, beta, out):
    import concourse.bass as bass
    from concourse import mybir
    from contextlib import ExitStack

    f32, f16, bf16 = mybir.dt.float32, mybir.dt.float16, mybir.dt.bfloat16
    i32, u16 = mybir.dt.int32, mybir.dt.uint16
    ALU, ACT, AX = mybir.AluOpType, mybir.ActivationFunctionType, mybir.AxisListType

    P = 128
    N, D = x.shape
    DA = W2.shape[0]
    T = -(-N // P)
    NP = T * P
    TAIL = N - (T - 1) * P
    assert T % 2 == 0 and D == 4 * P and DA == 64
    DC = D // P
    GB = 4
    NG = -(-T // GB)
    CHUNK = 512
    NCH = -(-NP // CHUNK)
    assert NG == NCH and NG % 2 == 1
    FS, RSC = 2.0 ** 10, 2.0 ** 14
    P_TOP, EPS = 0.9, 1e-5
    PASSES = (7, 11)
    RING = 4
    ALL_PASSES = 27
    TOP = RSC * 1.001
    BOTTOM = RSC * (1 - P_TOP) / NP * 0.95
    SPAN = math.log(TOP / BOTTOM)
    BIG = 1e30
    blocks = [range(g * GB, min(T, (g + 1) * GB)) for g in range(NG)]

    def ratio(k):
        return math.exp(SPAN / 2 ** (k + 1))

    h_plus_z = nc.dram_tensor("h_plus_z", [T, P, D], f32).ap()
    xa_next = nc.dram_tensor("xa_next", [T, P, 2 * D], f16).ap()
    q_dram = nc.dram_tensor("q_dram", [2, T, P, 3 * P], bf16).ap()
    k_dram = nc.dram_tensor("k_dram", [2, DA, 3, NP], bf16).ap()
    rt_dram = nc.dram_tensor("rt_dram", [T, P, T, 2 * P], f16).ap()

    with ExitStack() as ctx:
        def sb(name, shape, dt):
            return ctx.enter_context(nc.sbuf_tensor(name, shape, dt))

        def ps(name, shape):
            return ctx.enter_context(nc.psum_tensor(name, shape, f32))

        def sem(name):
            return ctx.enter_context(nc.semaphore(name))

        XA = sb("XA", [P, T, 2 * D], f16)
        XBf = sb("XBf", [P, T, D], f32)
        XB = XBf[:, :, :].bitcast(f16)
        K12, K13 = sb("K12", [P, NP], bf16), sb("K13", [P, NP], bf16)
        w2, qf = sb("w2", [DA, P], f32)[:, :], sb("qf", [DA, P], f32)[:, :]
        U1 = sb("U1", [P, DC, D], f32)
        U2 = sb("U2", [P, DC, D], f32)
        E = [sb(f"E{i}", [P, NP], f32) for i in range(2)]
        HALF = NP // 2
        masked = sb("masked", [P, HALF], f32)
        count = masked[:, :].bitcast(u16)
        choice = masked[:, :].bitcast(bf16)
        AD = sb("AD", [P, NP], f32)
        RT = AD[:, :].bitcast(f16).rearrange("p (b c) -> p b c", c=2 * P)
        ring = [sb(f"ring{i}", [P, GB, 2 * P], f16) for i in range(RING)]
        XN = [sb(f"XN{i}", [P, D], f32) for i in range(2)]
        xT = sb("xT", [P, DC, P], f32)
        zt = sb("zt", [P, D], f32)
        xah = sb("xah", [P, 2 * D], f16)
        w13 = sb("w13", [P, DC, 2 * DA], f32)
        ident = sb("ident", [P, P], f32)
        minus_eye = sb("minus_eye", [P, P], f16)
        qs = [sb(f"qs{i}", [P, 3, P], bf16) for i in range(2)]
        qk_parts = sb("qk_parts", [P, 3, P], bf16)
        qk = sb("qk", [P, P], f32)
        mv = sb("mv", [P, T, 2], f32)
        stdev = sb("stdev", [P, 32], f32)
        rstd = stdev[:, 0:T]
        cols = sb("cols", [P, 80], f32)
        flag_i = sb("flag_i", [P, 1], i32)
        names = ["neg_max", "goal", "lo", "hi", "t", "mass", "mass_hi", "up", "far", "v_star", "v_more",
                 "mass_gt", "reach", "bad", "quota", "below", "gap", "kept", "row_sum", "row_scale",
                 "eps", "tmp", "tmp2"]
        assert len(names) <= 24
        col = {n: cols[:, i:i + 1] for i, n in enumerate(names)}
        nb = [cols[:, 24 + i:25 + i] for i in range(2)]
        S = [cols[:, 26 + i:27 + i] for i in range(2)]
        rinv = [cols[:, 28 + i:29 + i] for i in range(2)]
        v8, cum8, w8 = cols[:, 32:40], cols[:, 40:48], cols[:, 48:56]
        mx8 = cols[:, 56:56 + NCH]
        v16 = cols[:, 64:80]
        flags = sb("flags", [P, 32], f32)
        flagsT = stdev
        st6, moments = w8[:, 0:6], cols[:, 30:32]
        halving = sb("halving", [P, ALL_PASSES], f32)

        pL = [ps(f"pL{i}", [P, CHUNK]) for i in range(2)]
        pT = [ps(f"pT{i}", [P, GB, P]) for i in range(2)]
        pR, pA, pZ = ps("pR", [P, D]), ps("pA", [P, D]), ps("pZ", [P, D])
        pX = ps("pX", [P, DC, P])

        x_in, w_in, k_in, xa_in = sem("x_in"), sem("w_in"), sem("k_in"), sem("xa_in")
        q_in = [sem("q_in0"), sem("q_in1")]
        z_in, adj_in, rt_in = sem("z_in"), sem("adj_in"), sem("rt_in")
        ident_made, consts_made = sem("ident_made"), sem("consts_made")
        stats_made, root_made = sem("stats_made"), sem("root_made")
        h_made, h_hi = sem("h_made"), sem("h_hi")
        h_stored = [sem("h_stored0"), sem("h_stored1")]
        logits_made, logits_taken = sem("logits_made"), sem("logits_taken")
        max_made, exp_made, mask_made = sem("max_made"), sem("exp_made"), sem("mask_made")
        turned, hi_made, hi_taken = sem("turned"), sem("hi_made"), sem("hi_taken")
        lo_left, used = sem("lo_left"), sem("used")
        RT_used = sem("RT_used")
        slot_stored = [sem(f"slot_stored{i}") for i in range(RING)]
        adj_eye, adj_summed, adj_recip, adj_scaled = sem("adj_eye"), sem("adj_summed"), sem("adj_recip"), sem("adj_scaled")
        xnR_made, xnA_made = sem("xnR_made"), sem("xnA_made")
        lo_made = sem("lo_made")
        x_turned, xT_made = sem("x_turned"), sem("xT_made")
        z_added, z_taken = sem("z_added"), sem("z_taken")
        qk_made, qf_made, q2_made, q2_taken = sem("qk_made"), sem("qf_made"), sem("q2_made"), sem("q2_taken")
        parts_made, split = sem("parts_made"), sem("split")
        z_stored, xa_stored, qk_stored = sem("z_stored"), sem("xa_stored"), sem("qk_stored")
        gb_made, gb_taken, ones_made = sem("gb_made"), sem("gb_taken"), sem("ones_made")
        y_in = [sem("y_in0"), sem("y_in1")]
        y_scaled, y_done = sem("y_scaled"), sem("y_done")
        out_stored = [sem("out_stored0"), sem("out_stored1")]

        block = ctx.enter_context(nc.Block())

        def tiles(engine, body):
            with engine.Fori(0, T // 2 - 1) as j:
                body(j * 2, j, 0, False)
                body(j * 2 + 1, j, 1, False)
            body(T - 2, T // 2 - 1, 0, False)
            body(T - 1, T // 2 - 1, 1, True)

        L = (2 * NG, NG)

        def group(s, i, par, q):
            n = s * T * L[0] + i * L[s] + q
            slot = q % RING
            back = q - RING if q >= RING else max(p for p in range(L[s]) if p % RING == slot) - L[s]
            bank = (par * L[s] + q) % 2
            return n, slot, bank, n - q + back + 1

        def stores_of(slot, upto):
            return sum(q % RING == slot for q in range(min(upto, NG)))

        @block.sync
        def _(sp):
            full = (T - 1) * P
            sp.wait_ge(consts_made, 1)
            sp.dma_start(XBf[:, 0:T - 1, :], x[0:full, :].rearrange("(t p) d -> p t d", p=P)).then_inc(x_in, 16)
            sp.dma_start(XBf[0:TAIL, T - 1, :], x[full:N, :]).then_inc(x_in, 16)
            sp.dma_start(w13[:, :, 0:DA], W1.rearrange("(c p) a -> p c a", p=P)).then_inc(w_in, 16)
            sp.dma_start(w13[:, :, DA:2 * DA], W3.rearrange("(c p) a -> p c a", p=P)).then_inc(w_in, 16)
            sp.dma_start(w2[:, 0:DA], W2).then_inc(w_in, 16)
            sp.dma_start(U1[:, :, :], U1_0.rearrange("(c p) a -> p c a", p=P)).then_inc(w_in, 16)
            sp.dma_start(U2[:, :, :], U2_0.rearrange("(c p) a -> p c a", p=P)).then_inc(w_in, 16)
            sp.dma_start(AD[:, 0:N], adj[0:P, :]).then_inc(adj_in, 16)

            def store_qk(s, i, n):
                sp.wait_ge(parts_made, n + 2)
                q_rows = q_dram[s, bass.ds(i, 1), :, :].rearrange("o r c -> (o r) c")
                sp.dma_start(q_rows[0:DA, :], qk_parts[0:DA, :, :].rearrange("r a c -> r (a c)")).then_inc(qk_stored, 16)
                sp.dma_start(q_rows[DA:P, 0:2 * P], qk_parts[0:DA, 0:2, :].rearrange("r a c -> r (a c)")).then_inc(qk_stored, 16)
                sp.dma_start(q_rows[DA:P, 2 * P:3 * P], qk_parts[0:DA, 0, :]).then_inc(qk_stored, 16)
                sp.dma_start(k_dram[s, :, :, bass.ds(i * P, P)], qk_parts[DA:P, :, :]).then_inc(qk_stored, 16)

            def phase0(i, j, par):
                sp.wait_ge(h_made, i + 1)
                sp.dma_start(h_plus_z[bass.ds(i, 1), :, :].rearrange("o p d -> (o p) d"), XN[par][:, :]).then_inc(h_stored[par], 16)
                store_qk(0, i, i)

            with sp.Fori(0, T // 2) as j:
                phase0(j * 2, j, 0)
                phase0(j * 2 + 1, j, 1)
            for par in range(2):
                sp.wait_ge(h_stored[par], 16 * (T // 2))

            def load_q(s, i, par):
                sp.dma_start(qs[par][:, :, :].rearrange("r a c -> r (a c)"),
                             q_dram[s, bass.ds(i, 1), :, :].rearrange("o r c -> (o r) c")).then_inc(q_in[par], 16)

            def tile(s, i, j, par, last, last_pair):
                g = s * T + i
                if not last_pair:
                    sp.wait_ge(logits_made, (g + 1) * NCH)
                    load_q(s, i + 2, par)
                sp.wait_ge(z_stored, 16 * (g + 1))
                sp.dma_start(zt[:, :], h_plus_z[bass.ds(i, 1), :, :].rearrange("o p d -> (o p) d")).then_inc(z_in, 16)
                if s == 0:
                    for q, bl in enumerate(blocks):
                        n, slot, _, _ = group(s, i, par, q)
                        sp.wait_ge(lo_left, n + 3)
                        sp.dma_start(rt_dram[bass.ds(i, 1), :, bl[0]:bl[-1] + 1, :].rearrange("o p b c -> (o p) b c"),
                                     ring[slot][:, 0:len(bl), :]).then_inc(slot_stored[slot], 16)
                    if not last:
                        sp.wait_ge(turned, group(s, i, par, NG - 1)[0] + 1)
                        if last_pair:
                            sp.dma_start(AD[0:TAIL, 0:N], adj[full:N, :]).then_inc(adj_in, 16)
                        else:
                            sp.dma_start(AD[:, 0:N], adj[bass.ds((i + 1) * P, P), :]).then_inc(adj_in, 16)
                    sp.wait_ge(xnA_made, g + 2)
                    sp.wait_ge(lo_made, T + 2 * (i + 1))
                    sp.dma_start(xa_next[bass.ds(i, 1), :, :].rearrange("o p d -> (o p) d"), xah[:, :]).then_inc(xa_stored, 16)
                    store_qk(1, i, T + i)
                elif not last:
                    sp.wait_ge(RT_used, i + 1)
                    sp.dma_start(RT, rt_dram[bass.ds(i + 1, 1), :, :, :].rearrange("o p b c -> (o p) b c")).then_inc(rt_in, 16)
                sp.wait_ge(z_taken, g + 2)
                sp.dma_start(h_plus_z[bass.ds(i, 1), :, :].rearrange("o p d -> (o p) d"), zt[:, :]).then_inc(z_stored, 16)

            for s in range(2):
                sp.wait_ge(qk_stored, 64 + 64 * T * (s + 1))
                if s == 1:
                    sp.wait_ge(xa_stored, 16 * (T + 1))
                    sp.wait_ge(used, T * L[0] + RING)
                    sp.wait_ge(z_added, 2 * T)
                    sp.wait_ge(z_stored, 16 * (T + 1))
                    for slot in range(RING):
                        sp.wait_ge(slot_stored[slot], 16 * (T * stores_of(slot, NG) + 1))
                for rows, part, K in ((0, 0, K12), (DA, 1, K12), (0, 0, K13), (DA, 2, K13)):
                    sp.dma_start(K[rows:rows + DA, :], k_dram[s, :, part, :]).then_inc(k_in, 16)
                for par in range(2):
                    load_q(s, par, par)
                if s == 1:
                    sp.dma_start(RT, rt_dram[0, :, :, :]).then_inc(rt_in, 16)
                    for half in range(2):
                        a, b = half * T // 2, (half + 1) * T // 2
                        sp.dma_start(XA[:, a:b, :], xa_next[a:b, :, :].rearrange("t p d -> p t d")).then_inc(xa_in, 16)
                    sp.dma_start(U1[:, :, :], U1_1.rearrange("(c p) a -> p c a", p=P)).then_inc(w_in, 16)
                    sp.dma_start(U2[:, :, :], U2_1.rearrange("(c p) a -> p c a", p=P)).then_inc(w_in, 16)
                with sp.Fori(0, T // 2 - 1) as j:
                    tile(s, j * 2, j, 0, False, False)
                    tile(s, j * 2 + 1, j, 1, False, False)
                tile(s, T - 2, T // 2 - 1, 0, False, True)
                tile(s, T - 1, T // 2 - 1, 1, True, True)

            sp.wait_ge(z_stored, 16 * (2 * T + 1))
            sp.wait_ge(mask_made, 2 * T)
            sp.wait_ge(used, T * (L[0] + L[1]) + RING)
            sp.wait_ge(z_added, 4 * T)
            sp.dma_start(U1[0:1, 0, :], gamma.rearrange("(o d) -> o d", o=1)).then_inc(w_in, 16)
            sp.dma_start(U1[0:1, 1, :], beta.rearrange("(o d) -> o d", o=1)).then_inc(w_in, 16)

            def last_phase(i, j, par, rows, x_rows):
                sp.wait_ge(out_stored[par], 16 * (j + 1))
                sp.dma_start(E[par][:, 0:D], h_plus_z[bass.ds(i, 1), :, :].rearrange("o p d -> (o p) d")).then_inc(y_in[par], 16)
                sp.dma_start(E[par][0:rows, D:2 * D], x_rows).then_inc(y_in[par], 16)

            def last_store(i, par, rows, out_rows):
                sp.wait_ge(y_done, i + 1)
                sp.dma_start(out_rows, E[par][0:rows, 0:D]).then_inc(out_stored[par], 16)

            with sp.Fori(0, T // 2 - 1) as j:
                for par in range(2):
                    i = j * 2 + par
                    last_phase(i, j, par, P, x[bass.ds(i * P, P), :])
                for par in range(2):
                    i = j * 2 + par
                    last_store(i, par, P, out[bass.ds(i * P, P), :])
            j = T // 2 - 1
            last_phase(T - 2, j, 0, P, x[(T - 2) * P:(T - 1) * P, :])
            last_phase(T - 1, j, 1, TAIL, x[full:N, :])
            last_store(T - 2, 0, P, out[(T - 2) * P:(T - 1) * P, :])
            last_store(T - 1, 1, TAIL, out[full:N, :])
            for par in range(2):
                sp.wait_ge(out_stored[par], 16 * (T // 2 + 1))

        @block.gpsimd
        def _(pool):
            nc.gpsimd.memset(ident[:, :], 0.0).then_inc(ident_made, 1)
            pool.wait_ge(ident_made, 1)
            nc.gpsimd.affine_select(out=ident[:, :], in_=ident[:, :], compare_op=ALU.not_equal, fill=1.0, base=0,
                                    pattern=[[-1, P]], channel_multiplier=1).then_inc(ident_made, 1)
            pool.wait_ge(ident_made, 2)
            nc.gpsimd.tensor_scalar(minus_eye[:, :], ident[:, :], -1.0, 0.0, ALU.mult, ALU.add).then_inc(ident_made, 1)

            def make_parts(n):
                pool.wait_ge(q2_taken, n + 1)
                nc.gpsimd.tensor_tensor(qk[:, :], qk[:, :], qk_parts[:, 0, :], ALU.subtract)
                pool.drain()
                nc.gpsimd.tensor_copy(qk_parts[:, 1, :], qk[:, :])
                pool.drain()
                nc.gpsimd.tensor_tensor(qk_parts[:, 2, :], qk[:, :], qk_parts[:, 1, :], ALU.subtract).then_inc(parts_made, 1)

            def phase0(i, par):
                pool.wait_ge(h_made, i + 1)
                pool.wait_ge(h_hi, i + 1)
                nc.gpsimd.tensor_tensor(XA[:, bass.ds(i, 1), D:2 * D].rearrange("p o d -> p (o d)"), XN[par][:, :],
                                        XA[:, bass.ds(i, 1), 0:D].rearrange("p o d -> p (o d)"),
                                        ALU.subtract).then_inc(lo_made, 1)
                make_parts(i)

            with pool.Fori(0, T // 2) as j:
                phase0(j * 2, 0)
                phase0(j * 2 + 1, 1)

            def add_eye(i):
                pool.wait_ge(adj_in, 16 * (i + 1))
                blk = AD[:, bass.ds(i * P, P)]
                nc.gpsimd.tensor_tensor(blk, blk, ident[:, :], ALU.add).then_inc(adj_eye, 1)

            add_eye(0)

            def tile0(i, j, par, last):
                if not last:
                    add_eye(i + 1)
                pool.wait_ge(xnR_made, i + 2)
                nc.gpsimd.tensor_tensor(XB[:, bass.ds(i, 1), D:2 * D].rearrange("p o d -> p (o d)"), XN[0][:, :],
                                        XB[:, bass.ds(i, 1), 0:D].rearrange("p o d -> p (o d)"),
                                        ALU.subtract).then_inc(lo_made, 1)
                pool.wait_ge(xnA_made, i + 2)
                nc.gpsimd.tensor_tensor(xah[:, D:2 * D], XN[1][:, :], xah[:, 0:D], ALU.subtract).then_inc(lo_made, 1)
                make_parts(T + i)

            tiles(pool, tile0)

            def last_phase(i, j, par):
                pool.wait_ge(y_scaled, i + 1)
                pool.wait_ge(gb_taken, 2)
                y, xx = E[par][:, 0:D], E[par][:, D:2 * D]
                nc.gpsimd.tensor_tensor(xx, xx, U1[:, 3, :], ALU.add)
                pool.drain()
                nc.gpsimd.tensor_tensor(y, y, xx, ALU.add).then_inc(y_done, 1)

            with pool.Fori(0, T // 2) as j:
                last_phase(j * 2, j, 0)
                last_phase(j * 2 + 1, j, 1)

        @block.scalar
        def _(act):
            act.wait_ge(stats_made, 1)
            nc.scalar.activation(rstd[:, :], mv[:, :, 1], ACT.Sqrt, bias=col["eps"]).then_inc(root_made, 1)

            def take_xT(n):
                act.wait_ge(x_turned, n + 1)
                nc.scalar.activation(xT[:, :, :], pX[:, :, :], ACT.Copy).then_inc(xT_made, 1)

            def take_qk(n):
                act.wait_ge(qk_made, n + 1)
                act.wait_ge(parts_made, n + 1)
                nc.scalar.activation(qf, pX[0:DA, 0, :], ACT.Copy)
                nc.scalar.activation(qk[DA:2 * DA, :], pX[DA:2 * DA, 0, :], ACT.Copy)
                act.wait_ge(qk_stored, 64 * (n + 1))
                nc.scalar.activation(qk_parts[DA:2 * DA, 0, :], pX[DA:2 * DA, 0, :], ACT.Copy).then_inc(qf_made, 1)
                act.wait_ge(q2_made, n + 1)
                nc.scalar.activation(qk_parts[0:DA, 0, :], pX[0:DA, 1, :], ACT.Copy)
                nc.scalar.activation(qk[0:DA, :], pX[0:DA, 1, :], ACT.Copy).then_inc(q2_taken, 1)

            def phase0(i, par):
                act.wait_ge(h_made, i + 1)
                nc.scalar.activation(XA[:, bass.ds(i, 1), 0:D].rearrange("p o d -> p (o d)"), XN[par][:, :], ACT.Copy).then_inc(h_hi, 1)
                take_xT(i)
                take_qk(i)

            with act.Fori(0, T // 2) as j:
                phase0(j * 2, 0)
                phase0(j * 2 + 1, 1)

            def exp(s, i, par):
                act.wait_ge(max_made, s * T + i + 1)
                nc.scalar.activation(E[par][:, 0:N], E[par][:, 0:N], ACT.Exp, bias=nb[par], scale=1.0 / FS ** 2,
                                     accum_out=S[par]).then_inc(exp_made, 1)

            def adj_sum(i):
                act.wait_ge(adj_eye, i + 1)
                nc.scalar.activation(AD[:, :], AD[:, :], ACT.Copy, accum_out=col["row_sum"]).then_inc(adj_summed, 1)

            def adj_scale(i):
                act.wait_ge(adj_recip, i + 1)
                nc.scalar.activation(AD[:, :], AD[:, :], ACT.Copy, scale=col["row_scale"]).then_inc(adj_scaled, 1)

            def hi_part(s, i, j, par, q):
                n, slot, bank, free = group(s, i, par, q)
                act.wait_ge(turned, n + 1)
                act.wait_ge(used, free + RING)
                if s == 0:
                    act.wait_ge(slot_stored[slot], 16 * (i * stores_of(slot, NG) + stores_of(slot, q) + 1))
                m = len(blocks[q % NG])
                nc.scalar.activation(ring[slot][:, 0:m, 0:P], pT[bank][:, 0:m, :], ACT.Copy).then_inc(hi_made, 1)

            def lo_part(s, i, j, par, q):
                n, slot, bank, _ = group(s, i, par, q)
                act.wait_ge(hi_taken, n + 1)
                m = len(blocks[q % NG])
                nc.scalar.activation(ring[slot][:, 0:m, P:2 * P], pT[bank][:, 0:m, :], ACT.Copy).then_inc(lo_left, 1)

            def tile(s, i, j, par, last):
                g = s * T + i
                for q in range(L[s] + 1):
                    if q < L[s]:
                        hi_part(s, i, j, par, q)
                    if q >= 1:
                        lo_part(s, i, j, par, q - 1)
                    if s == 0 and not last and q == NG + min(3, NG - 1):
                        adj_sum(i + 1)
                if s == 0:
                    act.wait_ge(used, group(s, i, par, NG - 1)[0] + 1 + RING)
                else:
                    act.wait_ge(RT_used, i + 1)
                act.wait_ge(x_turned, T + 2 * g)
                if s == 0:
                    act.wait_ge(lo_made, T + 2 * i)
                    nc.scalar.activation(XB[:, bass.ds(i, 1), 0:D].rearrange("p o d -> p (o d)"), pR[:, :], ACT.Copy,
                                         scale=1.0 / RSC)
                nc.scalar.activation(XN[0][:, :], pR[:, :], ACT.Copy, scale=1.0 / RSC).then_inc(xnR_made, 1)
                act.wait_ge(used, group(s, i, par, L[s] - 1)[0] + 1 + RING)
                if s == 0:
                    act.wait_ge(xa_stored, 16 * (i + 1))
                    nc.scalar.activation(xah[:, 0:D], pA[:, :], ACT.Copy, scale=rinv[par])
                nc.scalar.activation(XN[1][:, :], pA[:, :], ACT.Copy, scale=rinv[par]).then_inc(xnA_made, 1)
                if s == 0:
                    act.wait_ge(qk_made, T + i)
                else:
                    act.wait_ge(z_added, 2 * g)
                take_xT(T + 2 * g)
                act.wait_ge(z_added, 2 * g + 1)
                take_xT(T + 2 * g + 1)
                if s == 0:
                    take_qk(T + i)
                    if not last:
                        adj_scale(i + 1)
                if isinstance(i, int):
                    return
                exp(s, i + 2, par)

            adj_sum(0)
            adj_scale(0)
            for s in range(2):
                if s == 1:
                    for slot in range(RING):
                        act.wait_ge(slot_stored[slot], 16 * (T * stores_of(slot, NG) + 1))
                exp(s, 0, 0)
                exp(s, 1, 1)
                tiles(act, lambda i, j, par, last: tile(s, i, j, par, last))

            act.wait_ge(stats_made, 2)
            nc.scalar.activation(rstd[:, :], mv[:, :, 1], ACT.Sqrt, bias=col["eps"]).then_inc(root_made, 1)
            act.wait_ge(gb_made, 2)
            nc.scalar.activation(U1[:, 2, :], pR[:, :], ACT.Copy).then_inc(gb_taken, 1)
            nc.scalar.activation(U1[:, 3, :], pA[:, :], ACT.Copy).then_inc(gb_taken, 1)

        @block.vector
        def _(dve):
            nc.vector.memset(w2, 0.0)
            nc.vector.memset(XBf[:, T - 1, :], 0.0)
            dve.drain().then_inc(consts_made, 1)
            for k in range(ALL_PASSES):
                nc.vector.memset(halving[:, k:k + 1], ratio(k))
            nc.vector.memset(flags[:, :], 0.0)
            nc.vector.memset(col["eps"], EPS)
            nc.vector.memset(E[0][:, N:NP], 0.0)
            nc.vector.memset(E[1][:, N:NP], 0.0)
            nc.vector.memset(AD[:, N:NP], 0.0)
            dve.drain()
            for free, n in ((logits_taken, 2), (lo_left, 2), (used, RING), (parts_made, 1),
                            *((x, 16) for x in slot_stored), (xnR_made, 1), (xnA_made, 1), (z_taken, 1), (z_stored, 16),
                            (xa_stored, 16), (qk_stored, 64), (out_stored[0], 16), (out_stored[1], 16)):
                dve.sem_inc(free, n)

            dve.wait_ge(x_in, 32)

            def stats(i, src):
                nc.vector.bn_stats(st6, src)
                dve.drain()
                nc.vector.bn_aggr(moments, st6)
                dve.drain()
                nc.vector.tensor_copy(mv[:, bass.ds(i, 1), :].rearrange("p o c -> p (o c)"), moments)

            with dve.Fori(0, T) as i:
                stats(i, XBf[:, bass.ds(i, 1), :].rearrange("p o d -> p (o d)"))
            dve.drain().then_inc(stats_made, 1)
            dve.wait_ge(root_made, 1)
            nc.vector.reciprocal(rstd[:, :], rstd[:, :])
            dve.drain()

            def phase0(i, j, par, first):
                xi = XBf[:, bass.ds(i, 1), :].rearrange("p o d -> p (o d)")
                nc.vector.tensor_scalar(xi, xi, mv[:, bass.ds(i, 1), 0], rstd[:, bass.ds(i, 1)], ALU.subtract, ALU.mult)
                dve.drain()
                if not first:
                    dve.wait_ge(x_turned, i - 1)
                    dve.wait_ge(h_hi, i - 1)
                    dve.wait_ge(lo_made, i - 1)
                    dve.wait_ge(h_stored[par], 16 * j)
                nc.vector.tensor_scalar(XN[par][:, :], xi, 0.0, FS, ALU.max, ALU.mult).then_inc(h_made, 1)

            phase0(0, 0, 0, True)
            phase0(1, 0, 1, True)
            with dve.Fori(1, T // 2) as j:
                phase0(j * 2, j, 0, False)
                phase0(j * 2 + 1, j, 1, False)

            def take_logits(s, i, par):
                g = s * T + i
                if not isinstance(i, int):
                    dve.wait_ge(turned, group(s, i - 2, par, L[s] - 1)[0] + 1)
                elif s == 1:
                    dve.wait_ge(turned, T * L[0])
                for c in range(NCH):
                    w = min(CHUNK, N - c * CHUNK)
                    dve.wait_ge(logits_made, g * NCH + c + 1)
                    nc.vector.tensor_scalar(E[par][:, c * CHUNK:c * CHUNK + w], pL[(par + c) % 2][:, 0:w], 1.0, None,
                                            ALU.mult, ALU.max, accum_out=mx8[:, c:c + 1]).then_inc(logits_taken, 1)
                dve.drain()
                nc.vector.tensor_reduce(col["neg_max"], mx8, AX.X, ALU.max)
                dve.drain()
                nc.vector.tensor_scalar(nb[par], col["neg_max"], -1.0 / FS ** 2, math.log(RSC), ALU.mult, ALU.add).then_inc(max_made, 1)

            def light_pass(par, k):
                c, step_up = col, ratio(k + 1)
                nc.vector.scalar_tensor_tensor(out=choice[:, 0:N], in0=E[par][:, 0:N], scalar=c["t"], in1=E[par][:, 0:N],
                                               op0=ALU.is_gt, op1=ALU.mult, accum_out=c["mass"])
                dve.drain()
                nc.vector.tensor_scalar(c["up"], c["mass"], c["goal"], step_up - 1 / step_up, ALU.is_ge, ALU.mult)
                dve.drain()
                nc.vector.scalar_tensor_tensor(out=c["t"], in0=c["up"], scalar=1 / step_up, in1=c["t"], op0=ALU.add, op1=ALU.mult)
                dve.drain()

            def full_pass(par):
                c = col
                nc.vector.scalar_tensor_tensor(out=choice[:, 0:N], in0=E[par][:, 0:N], scalar=c["t"], in1=E[par][:, 0:N],
                                               op0=ALU.is_gt, op1=ALU.mult, accum_out=c["mass"])
                dve.drain()
                nc.vector.tensor_scalar(c["up"], c["mass"], c["goal"], None, ALU.is_ge)
                dve.drain()
                nc.vector.scalar_tensor_tensor(out=c["lo"], in0=c["up"], scalar=c["t"], in1=c["lo"], op0=ALU.mult, op1=ALU.max)
                nc.vector.scalar_tensor_tensor(out=c["far"], in0=c["up"], scalar=BIG, in1=c["t"], op0=ALU.mult, op1=ALU.add)
                dve.drain()
                nc.vector.tensor_tensor(c["hi"], c["hi"], c["far"], ALU.min)
                dve.drain()

            def eight_below(par):
                c, e = col, E[par]
                for h, (a, b) in enumerate(((0, HALF), (HALF, N))):
                    nc.vector.scalar_tensor_tensor(out=masked[:, 0:b - a], in0=e[:, a:b], scalar=c["hi"], in1=e[:, a:b],
                                                   op0=ALU.is_le, op1=ALU.mult, accum_out=c["tmp"] if h == 0 else c["tmp2"])
                    dve.drain()
                    nc.vector.max(v16[:, 8 * h:8 * h + 8], masked[:, 0:b - a])
                    dve.drain()
                nc.vector.max(v8, v16)
                nc.vector.tensor_tensor(c["mass_hi"], c["tmp"], c["tmp2"], ALU.add)
                dve.drain()
                nc.vector.tensor_tensor(c["mass_hi"], S[par], c["mass_hi"], ALU.subtract)
                dve.drain()

            def threshold(par):
                c = col
                nc.vector.tensor_tensor_scan(cum8, v8, v8, c["mass_hi"], ALU.add, ALU.max)
                dve.drain()
                nc.vector.tensor_scalar(w8, cum8, c["goal"], None, ALU.is_ge)
                dve.drain()
                nc.vector.tensor_tensor(cum8, w8, v8, ALU.mult)
                dve.drain()
                nc.vector.tensor_reduce(c["tmp"], cum8, AX.X, ALU.max)
                dve.drain()
                nc.vector.tensor_tensor(c["v_star"], c["tmp"], v8[:, 7:8], ALU.max)
                dve.drain()
                nc.vector.scalar_tensor_tensor(out=cum8, in0=v8, scalar=c["v_star"], in1=v8, op0=ALU.is_gt, op1=ALU.mult,
                                               accum_out=c["v_more"])
                dve.drain()
                nc.vector.tensor_tensor(c["mass_gt"], c["mass_hi"], c["v_more"], ALU.add)
                dve.drain()

            def flag_plain():
                c = col
                nc.vector.tensor_reduce(c["tmp"], w8, AX.X, ALU.add)
                nc.vector.tensor_scalar(cum8, v8, c["v_star"], 0.0, ALU.is_ge, ALU.add, accum_out=c["tmp2"])
                dve.drain()
                nc.vector.tensor_tensor(c["up"], c["tmp"], c["tmp2"], ALU.add)
                nc.vector.tensor_scalar(c["far"], c["tmp"], 2.0, None, ALU.is_lt)
                dve.drain()
                nc.vector.scalar_tensor_tensor(out=flags[:, 0:1], in0=c["up"], scalar=9.0, in1=c["far"],
                                               op0=ALU.not_equal, op1=ALU.max)
                dve.drain()

            def count_equals(par):
                c, n = col, count[:, 0:N]
                nc.vector.tensor_scalar(n, E[par][:, 0:N], c["v_star"], None, ALU.is_equal)
                dve.drain()
                nc.vector.tensor_tensor_scan(n, n, n, 0.0, ALU.add, ALU.max)
                dve.drain()
                nc.vector.scalar_tensor_tensor(out=c["reach"], in0=count[:, N - 1:N], scalar=c["v_star"], in1=c["mass_gt"],
                                               op0=ALU.mult, op1=ALU.add)
                dve.drain()
                nc.vector.tensor_scalar(c["tmp"], c["reach"], c["goal"], None, ALU.is_lt)
                nc.vector.tensor_scalar(c["tmp2"], c["mass_gt"], c["goal"], None, ALU.is_ge)
                dve.drain()
                nc.vector.tensor_tensor(flags[:, 0:1], c["tmp"], c["tmp2"], ALU.max)
                dve.drain()

            def any_flag():
                c = col
                nc.vector.transpose(flagsT[:, :], flags[:, :])
                dve.drain()
                nc.vector.tensor_reduce(c["bad"], flagsT[:, :], AX.X, ALU.max)
                dve.drain()
                for q in range(4):
                    nc.vector.tensor_copy(w8[0:1, q:q + 1], c["bad"][32 * q:32 * q + 1, :])
                dve.drain()
                nc.vector.tensor_reduce(flag_i[0:1, :], w8[0:1, 0:4], AX.X, ALU.max)
                dve.drain()
                return dve.value_load(flag_i[0:1, 0:1], min_val=0, max_val=1)

            def search(s, i, par, after_passes):
                c = col
                e, flagged = E[par][:, 0:N], choice[:, 0:N]
                nc.vector.memset(c["t"], BOTTOM * ratio(0))
                dve.wait_ge(exp_made, s * T + i + 1)
                nc.vector.tensor_scalar(c["goal"], S[par], P_TOP, None, ALU.mult)
                dve.drain()
                for k in range(PASSES[s]):
                    light_pass(par, k)
                nc.vector.tensor_scalar(c["hi"], c["t"], ratio(PASSES[s]) * (1 + 1e-6), None, ALU.mult)
                dve.drain()
                eight_below(par)
                threshold(par)
                flag_plain()
                with dve.If(any_flag() != 0):
                    count_equals(par)
                    with dve.If(any_flag() != 0):
                        nc.vector.tensor_scalar(c["up"], c["reach"], c["goal"], None, ALU.is_ge)
                        nc.vector.tensor_scalar(c["below"], c["v_star"], 1.0 - 2.0 ** -24, None, ALU.mult)
                        dve.drain()
                        nc.vector.scalar_tensor_tensor(out=c["tmp"], in0=c["up"], scalar=BIG, in1=c["below"], op0=ALU.mult, op1=ALU.add)
                        dve.drain()
                        nc.vector.tensor_tensor(c["hi"], c["hi"], c["tmp"], ALU.min)
                        dve.drain()
                        eight_below(par)
                        threshold(par)
                        count_equals(par)
                        with dve.If(any_flag() != 0):
                            nc.vector.memset(c["lo"], BOTTOM)
                            nc.vector.memset(c["hi"], TOP)
                            dve.drain()
                            with dve.Fori(0, ALL_PASSES) as k:
                                nc.vector.tensor_tensor(c["t"], c["lo"], halving[:, bass.ds(k, 1)], ALU.mult)
                                dve.drain()
                                full_pass(par)
                            eight_below(par)
                            threshold(par)
                            count_equals(par)
                        with dve.Else():
                            dve.drain()
                        dve.drain()
                    with dve.Else():
                        dve.drain()
                    nc.vector.tensor_tensor(c["tmp"], c["goal"], c["mass_gt"], ALU.subtract)
                    nc.vector.reciprocal(c["tmp2"], c["v_star"])
                    nc.vector.tensor_scalar(c["below"], c["v_star"], 1.0 - 2.0 ** -24, None, ALU.mult)
                    dve.drain()
                    nc.vector.tensor_scalar(c["quota"], c["tmp"], c["tmp2"], 1.0, ALU.mult, ALU.add)
                    nc.vector.tensor_tensor(c["gap"], c["v_star"], c["below"], ALU.subtract)
                    dve.drain()
                    nc.vector.tensor_scalar(flagged, count[:, 0:N], c["quota"], c["gap"], ALU.is_ge, ALU.mult)
                    dve.drain()
                    nc.vector.scalar_tensor_tensor(out=flagged, in0=flagged, scalar=c["below"], in1=e, op0=ALU.add, op1=ALU.is_lt)
                    dve.drain()
                    nc.vector.scalar_tensor_tensor(out=e, in0=flagged, scalar=1.0, in1=e, op0=ALU.mult, op1=ALU.mult,
                                                   accum_out=c["kept"])
                    dve.drain()
                with dve.Else():
                    nc.vector.scalar_tensor_tensor(out=e, in0=e, scalar=c["v_star"], in1=e, op0=ALU.is_ge, op1=ALU.mult,
                                                   accum_out=c["kept"])
                    dve.drain()
                nc.vector.reciprocal(rinv[par], c["kept"]).then_inc(mask_made, 1)
                after_passes()

            def adj_recip_of(i):
                dve.wait_ge(adj_summed, i + 1)
                nc.vector.tensor_scalar(col["row_sum"], col["row_sum"], 1e-12, 1.0 / RSC, ALU.max, ALU.mult)
                dve.drain()
                nc.vector.reciprocal(col["row_scale"], col["row_sum"]).then_inc(adj_recip, 1)

            def tile(s, i, par, last):
                g = s * T + i
                if not last:
                    search(s, i + 1, 1 - par, lambda: adj_recip_of(i + 1) if s == 0 else None)
                if not isinstance(i, int):
                    take_logits(s, i + 2, par)
                dve.wait_ge(z_in, 16 * (g + 1))
                dve.wait_ge(z_added, 2 * (g + 1))
                nc.vector.tensor_tensor(zt[:, :], pZ[:, :], zt[:, :], ALU.add)
                dve.drain()
                if s == 1:
                    stats(i, zt[:, :])
                dve.drain().then_inc(z_taken, 1)

            adj_recip_of(0)
            for s in range(2):
                take_logits(s, 0, 0)
                take_logits(s, 1, 1)
                search(s, 0, 0, lambda: None)
                tiles(dve, lambda i, j, par, last: tile(s, i, par, last))

            nc.vector.memset(col["eps"], EPS * FS ** 2)
            nc.vector.memset(qf[0:1, :], 1.0).then_inc(ones_made, 1)
            dve.drain().then_inc(stats_made, 1)
            dve.wait_ge(root_made, 2)
            nc.vector.reciprocal(rstd[:, :], rstd[:, :])
            dve.drain()
            dve.wait_ge(gb_taken, 2)

            def last_phase(i, j, par):
                y = E[par][:, 0:D]
                dve.wait_ge(y_in[par], 32 * (j + 1))
                nc.vector.tensor_scalar(y, y, mv[:, bass.ds(i, 1), 0], rstd[:, bass.ds(i, 1)], ALU.subtract, ALU.mult)
                dve.drain()
                nc.vector.tensor_tensor(y, y, U1[:, 2, :], ALU.mult).then_inc(y_scaled, 1)

            with dve.Fori(0, T // 2) as j:
                last_phase(j * 2, j, 0)
                last_phase(j * 2 + 1, j, 1)

        @block.tensor
        def _(pe):
            pe.wait_ge(ident_made, 3)
            pe.wait_ge(w_in, 16 * 5)

            def turn_x(rows, n):
                for c in range(DC):
                    last = nc.tensor.transpose(pX[:, c, :], rows[:, c * P:(c + 1) * P], ident[:, :])
                last.then_inc(x_turned, 1)
                pe.wait_ge(xT_made, n + 1)

            def query_key(n):
                for c in range(DC):
                    last = nc.tensor.matmul(pX[:, 0, :], w13[:, c, :], xT[:, c, :], start=(c == 0), stop=(c == DC - 1))
                last.then_inc(qk_made, 1)
                pe.wait_ge(qf_made, n + 1)
                nc.tensor.matmul(pX[:, 1, :], w2, qf, start=True, stop=True).then_inc(q2_made, 1)
                pe.wait_ge(q2_taken, n + 1)

            def phase0(i, par):
                pe.wait_ge(h_made, i + 1)
                turn_x(XN[par], i)
                query_key(i)

            with pe.Fori(0, T // 2) as j:
                phase0(j * 2, 0)
                phase0(j * 2 + 1, 1)

            def logits(s, i, j, par):
                g = s * T + i
                pe.wait_ge(q_in[par], 16 * (s * (T // 2) + j + 1))
                for c in range(NCH):
                    w = min(CHUNK, NP - c * CHUNK)
                    pe.wait_ge(logits_taken, g * NCH + c + 1)
                    for a, K in enumerate((K12, K12, K13)):
                        last = nc.tensor.matmul(pL[(par + c) % 2][:, 0:w], qs[par][:, a, :], K[:, c * CHUNK:c * CHUNK + w],
                                                start=(a == 0), stop=(a == 2))
                    last.then_inc(logits_made, 1)

            def turn(s, i, par, q, src):
                n, _, bank, _ = group(s, i, par, q)
                pe.wait_ge(lo_left, n + 1)
                for b in blocks[q % NG]:
                    last = nc.tensor.matmul(pT[bank][:, b % GB, :], src[:, b * P:(b + 1) * P], ident[:, :],
                                            is_transpose=True, start=(b % GB == 0), stop=False, skip_group_check=True)
                last.then_inc(turned, 1)

            def take_hi(s, i, par, q):
                n, slot, bank, _ = group(s, i, par, q)
                m = len(blocks[q % NG])
                pe.wait_ge(hi_made, n + 1)
                nc.tensor.matmul(pT[bank][:, 0:m, :], minus_eye[:, :], ring[slot][:, 0:m, 0:P],
                                 start=False, stop=True, skip_group_check=True).then_inc(hi_taken, 1)

            def products(acc, weights, X, k, done):
                for b in blocks[k]:
                    whi, wlo = weights(b)
                    xhi, xlo = X[:, b, 0:D], X[:, b, D:2 * D]
                    nc.tensor.matmul(acc[:, :], whi, xhi, start=(b == 0), stop=False)
                    nc.tensor.matmul(acc[:, :], whi, xlo, start=False, stop=False)
                    last = nc.tensor.matmul(acc[:, :], wlo, xhi, start=False, stop=(b == T - 1))
                if done is not None:
                    last.then_inc(done, 1)

            def tile(s, i, j, par, last):
                g = s * T + i
                if s == 1:
                    pe.wait_ge(rt_in, 16 * (i + 1))
                    pe.wait_ge(xnR_made, g + 1)
                    for k in range(NG):
                        products(pR, lambda b: (RT[:, b, 0:P], RT[:, b, P:2 * P]), XB, k, RT_used if k == NG - 1 else None)
                for q in range(L[s] + 2):
                    if q < L[s]:
                        if s == 0 and q == 0:
                            pe.wait_ge(adj_scaled, i + 1)
                        if q == L[s] - NG:
                            pe.wait_ge(mask_made, g + 1)
                        turn(s, i, par, q, AD if q < L[s] - NG else E[par])
                    if 1 <= q <= L[s]:
                        take_hi(s, i, par, q - 1)
                    if q >= 2:
                        n, slot, _, _ = group(s, i, par, q - 2)
                        of_R = q - 2 < L[s] - NG
                        if q == 2 or q - 2 == L[s] - NG:
                            pe.wait_ge(xnR_made if of_R else xnA_made, g + 1)
                        pe.wait_ge(lo_left, n + 3)
                        products(pR if of_R else pA, lambda b: (ring[slot][:, b % GB, 0:P], ring[slot][:, b % GB, P:2 * P]),
                                 XA, (q - 2) % NG, used)
                pe.wait_ge(xnR_made, g + 2)
                turn_x(XN[0], T + 2 * g)
                pe.wait_ge(z_taken, g + 1)
                for c in range(DC):
                    last_z = nc.tensor.matmul(pZ[:, :], xT[:, c, :], U1[:, c, :], start=(c == 0), stop=False)
                last_z.then_inc(z_added, 1)
                pe.wait_ge(xnA_made, g + 2)
                turn_x(XN[1], T + 2 * g + 1)
                for c in range(DC):
                    last_z = nc.tensor.matmul(pZ[:, :], xT[:, c, :], U2[:, c, :], start=False, stop=(c == DC - 1))
                last_z.then_inc(z_added, 1)
                if s == 0:
                    query_key(T + i)
                if not isinstance(i, int):
                    logits(s, i + 2, j + 1, par)

            for s in range(2):
                pe.wait_ge(k_in, 64 * (s + 1))
                if s == 1:
                    pe.wait_ge(xa_in, 32)
                    pe.wait_ge(w_in, 16 * 7)
                    pe.wait_ge(lo_made, 3 * T)
                logits(s, 0, 0, 0)
                logits(s, 1, 0, 1)
                tiles(pe, lambda i, j, par, last: tile(s, i, j, par, last))

            pe.wait_ge(w_in, 16 * 9)
            pe.wait_ge(ones_made, 1)
            for k, acc in ((0, pR), (1, pA)):
                nc.tensor.matmul(acc[:, :], qf[0:1, :], U1[0:1, k, :], start=True, stop=True).then_inc(gb_made, 1)


_INS = ["x", "adj", "L0_gnn_W1", "L0_gnn_W2", "L0_gnn_W3", "L0_gnn_U1_0", "L0_gnn_U1_1", "L0_gnn_U2_0", "L0_gnn_U2_1",
        "L0_gnn_gamma", "L0_gnn_beta"]


def kernel(**inputs):
    import numpy as _np
    import concourse.bacc as _bacc
    from concourse import mybir as _mybir
    from concourse.bass_utils import run_bass_kernel_spmd as _run

    nc = _bacc.Bacc("TRN2", target_bir_lowering=False, num_devices=1)
    arrays, args = {}, []
    for name in _INS:
        a = _np.ascontiguousarray(inputs[name])
        arrays[f"in_{name}_dram"] = a
        args.append(nc.dram_tensor(f"in_{name}_dram", a.shape, _mybir.dt.from_np(a.dtype), kind="ExternalInput").ap())
    shape = inputs["x"].shape
    args.append(nc.dram_tensor("out_dram", shape, _mybir.dt.float32, kind="ExternalOutput").ap())
    build_top_p_gnn(nc, *args)
    r = _run(nc, [arrays], core_ids=[0])
    return r.results[0]["out_dram"]
```

```python
import math


def build_top_p_gnn(nc, x, adj, W1, W2, W3, U1_0, U1_1, U2_0, U2_1, gamma, beta, out):
    import concourse.bass as bass
    from concourse import mybir
    from contextlib import ExitStack

    f32, f16, bf16 = mybir.dt.float32, mybir.dt.float16, mybir.dt.bfloat16
    i32, u16 = mybir.dt.int32, mybir.dt.uint16
    ALU, ACT, AX = mybir.AluOpType, mybir.ActivationFunctionType, mybir.AxisListType

    P = 128
    N, D = x.shape
    DA = W2.shape[0]
    T = -(-N // P)
    NP = T * P
    TAIL = N - (T - 1) * P
    assert T % 2 == 0 and D == 4 * P and DA == 64
    DC = D // P
    GB = 4
    NG = -(-T // GB)
    CHUNK = 512
    NCH = -(-NP // CHUNK)
    assert NG == NCH and NG % 2 == 1
    FS, RSC = 2.0 ** 10, 2.0 ** 14
    P_TOP, EPS = 0.9, 1e-5
    PASSES = (7, 10)
    LEVELS = 4
    TAKE = (5, 8)
    RING = 4
    ALL_PASSES = 27
    TOP = RSC * 1.001
    BOTTOM = RSC * 2 / NP
    LEAST = RSC * (1 - P_TOP) / NP * 0.95
    SPAN, WHOLE_SPAN = math.log(TOP / BOTTOM), math.log(TOP / LEAST)
    SLACK = 1e-6
    BIG = 1e30
    blocks = [range(g * GB, min(T, (g + 1) * GB)) for g in range(NG)]

    def ratio(k, span=SPAN):
        return math.exp(span / 2 ** (k + 1))

    h_plus_z = nc.dram_tensor("h_plus_z", [T, P, D], f32).ap()
    xa_next = nc.dram_tensor("xa_next", [T, P, 2 * D], f16).ap()
    q_dram = nc.dram_tensor("q_dram", [2, T, P, 3 * P], bf16).ap()
    k_dram = nc.dram_tensor("k_dram", [2, DA, 3, NP], bf16).ap()
    rt_dram = nc.dram_tensor("rt_dram", [T, P, T, 2 * P], f16).ap()

    with ExitStack() as ctx:
        def sb(name, shape, dt):
            return ctx.enter_context(nc.sbuf_tensor(name, shape, dt))

        def ps(name, shape):
            return ctx.enter_context(nc.psum_tensor(name, shape, f32))

        def sem(name):
            return ctx.enter_context(nc.semaphore(name))

        XA = sb("XA", [P, T, 2 * D], f16)
        XBf = sb("XBf", [P, T, D], f32)
        XB = XBf[:, :, :].bitcast(f16)
        K12, K13 = sb("K12", [P, NP], bf16), sb("K13", [P, NP], bf16)
        small = sb("small", [P, 5 * P], f32)
        w2, qf, qk = small[0:DA, 0:P], small[0:DA, P:2 * P], small[:, 2 * P:3 * P]
        qk_parts = small[:, 3 * P:5 * P].bitcast(bf16)[:, 0:3 * P].rearrange("r (a c) -> r a c", a=3)
        beta_rows = small[:, 0:D]
        U1 = sb("U1", [P, DC, D], f32)
        U2 = sb("U2", [P, DC, D], f32)
        E = [sb(f"E{i}", [P, NP], f32) for i in range(2)]
        HALF = NP // 2
        masked = sb("masked", [P, HALF], f32)
        count = masked[:, :].bitcast(u16)
        choice = masked[:, :].bitcast(bf16)
        unread = sb("unread", [P, N], mybir.dt.uint8)
        AD = sb("AD", [P, NP], f32)
        RT = AD[:, :].bitcast(f16).rearrange("p (b c) -> p b c", c=2 * P)
        ring = [sb(f"ring{i}", [P, GB, 2 * P], f16) for i in range(RING)]
        XN = [sb(f"XN{i}", [P, D], f32) for i in range(2)]
        xT = sb("xT", [P, DC, P], f32)
        zt = sb("zt", [P, D], f32)
        xah = sb("xah", [P, 2 * D], f16)
        x_rows = xah[:, :].bitcast(f32)
        w13 = sb("w13", [P, DC, 2 * DA], f32)
        gamma_rows = w13[:, :, :].rearrange("p c a -> p (c a)")
        ident = sb("ident", [P, P], f32)
        minus_eye = sb("minus_eye", [P, P], f16)
        qs = [sb(f"qs{i}", [P, 3, P], bf16) for i in range(2)]
        mv = sb("mv", [P, T, 2], f32)
        stdev = sb("stdev", [P, 32], f32)
        rstd = stdev[:, 0:T]
        cols = sb("cols", [P, 80], f32)
        flag_i = sb("flag_i", [P, 1], i32)
        names = ["neg_max", "goal", "lo", "hi", "t", "mass", "mass_hi", "up", "far", "v_star", "v_more",
                 "mass_gt", "reach", "bad", "quota", "below", "gap", "kept", "row_sum", "row_scale",
                 "eps", "eps_y", "tmp", "tmp2"]
        assert len(names) <= 24
        col = {n: cols[:, i:i + 1] for i, n in enumerate(names)}
        nb = [cols[:, 24 + i:25 + i] for i in range(2)]
        S = [cols[:, 26 + i:27 + i] for i in range(2)]
        rinv = [cols[:, 28 + i:29 + i] for i in range(2)]
        v8, cum8, w8 = cols[:, 32:40], cols[:, 40:48], cols[:, 48:56]
        mx8 = cols[:, 56:56 + NCH]
        v16 = cols[:, 64:80]
        flags = sb("flags", [P, 32], f32)
        flagsT = stdev
        st6, moments = w8[:, 0:6], cols[:, 30:32]
        more_cols = sb("more_cols", [P, 22], f32)
        S_part = [[more_cols[:, 2 * i + h:2 * i + h + 1] for h in range(2)] for i in range(2)]
        above_t, signs = [[more_cols[:, 4 + 2 * k + i:5 + 2 * k + i] for i in range(2)] for k in range(2)]
        t_of, minus_t = [[more_cols[:, 8 + 2 * k + i:9 + 2 * k + i] for i in range(2)] for k in range(2)]
        pool_goal, pool_mass, pool_up = [more_cols[:, 12 + k:13 + k] for k in range(3)]
        adj_part = [more_cols[:, 15 + h:16 + h] for h in range(2)]
        var_y, root_y, tmp_y, seed_y = [more_cols[:, 17 + k:18 + k] for k in range(4)]
        stage = [(E[i][:, 0:D].rearrange("p (c a) -> p c a", c=DC), E[i][0:DA, D:D + P], E[i][:, D + P:D + 2 * P],
                  E[i][:, D + 2 * P:D + 4 * P].bitcast(bf16)[:, 0:3 * P].rearrange("r (a c) -> r a c", a=3)) for i in range(2)]
        stage.append((xT, qf, qk, qk_parts))
        OWN = 2
        halving = sb("halving", [P, ALL_PASSES], f32)

        pL = [ps(f"pL{i}", [P, CHUNK]) for i in range(2)]
        pT = [ps(f"pT{i}", [P, GB, P]) for i in range(2)]
        pR, pA, pZ = ps("pR", [P, D]), ps("pA", [P, D]), ps("pZ", [P, D])
        pX = ps("pX", [P, DC, P])
        stage_ps = [pX, pR[:, :].rearrange("p (c a) -> p c a", c=DC), pX]

        x_in, w_in, k_in, xa_in = [sem(f"x_in{i}") for i in range(3)], sem("w_in"), sem("k_in"), sem("xa_in")
        U_in = sem("U_in")
        q_in = [sem("q_in0"), sem("q_in1")]
        z_in, adj_in, rt_in = sem("z_in"), sem("adj_in"), sem("rt_in")
        ident_made, consts_made = sem("ident_made"), sem("consts_made")
        stats_made, root_made = sem("stats_made"), sem("root_made")
        h_made, h_hi = sem("h_made"), sem("h_hi")
        h_stored = [sem("h_stored0"), sem("h_stored1")]
        logits_made, logits_taken = sem("logits_made"), sem("logits_taken")
        max_made, exp_made, mask_made = sem("max_made"), sem("exp_made"), sem("mask_made")
        sums_made, t_moved = sem("sums_made"), sem("t_moved")
        turned, hi_made, hi_taken = sem("turned"), sem("hi_made"), sem("hi_taken")
        lo_left, used = sem("lo_left"), sem("used")
        RT_used = sem("RT_used")
        slot_stored = [sem(f"slot_stored{i}") for i in range(RING)]
        adj_eye, adj_summed, adj_recip, adj_scaled = sem("adj_eye"), sem("adj_summed"), sem("adj_recip"), sem("adj_scaled")
        xnR_made, xnA_made = sem("xnR_made"), sem("xnA_made")
        lo_made = sem("lo_made")
        x_turned, xT_made = sem("x_turned"), sem("xT_made")
        z_added, z_taken = sem("z_added"), sem("z_taken")
        qk_made, qf_made, q2_made = sem("qk_made"), sem("qf_made"), sem("q2_made")
        q2_taken, parts_made = sem("q2_taken"), sem("parts_made")
        z_stored, xa_stored = sem("z_stored"), sem("xa_stored")
        qk_stored = [sem("qk_stored0"), sem("qk_stored1")]
        gb_in, x_rows_in = sem("gb_in"), sem("x_rows_in")
        y_done, out_stored = sem("y_done"), sem("out_stored")

        block = ctx.enter_context(nc.Block())

        def tiles(engine, body):
            with engine.Fori(0, T // 2 - 1) as j:
                body(j * 2, j, 0, False)
                body(j * 2 + 1, j, 1, False)
            body(T - 2, T // 2 - 1, 0, False)
            body(T - 1, T // 2 - 1, 1, True)

        def tiles_after_first(engine, body):
            body(0, 0, 0, True)
            body(1, 0, 1, False)
            with engine.Fori(1, T // 2 - 1) as j:
                body(j * 2, j, 0, False)
                body(j * 2 + 1, j, 1, False)
            body(T - 2, T // 2 - 1, 0, False)
            body(T - 1, T // 2 - 1, 1, False)

        def has_more(i):
            return not isinstance(i, int) or i < T - 2

        PAIRS = T // 2
        J1 = PAIRS // 2
        x_chunks = (range(0, 4), range(4, 2 * J1 + 2), range(2 * J1 + 2, T - 1))

        SUM_AT = max(0, min(2, NG - 5))
        L = (2 * NG, NG)

        def group(s, i, par, q):
            n = s * T * L[0] + i * L[s] + q
            slot = q % RING
            back = q - RING if q >= RING else max(p for p in range(L[s]) if p % RING == slot) - L[s]
            bank = (par * L[s] + q) % 2
            return n, slot, bank, n - q + back + 1

        def stores_of(slot, upto=2 * NG):
            return sum(q % RING == slot for q in range(NG, upto))

        @block.sync
        def _(sp):
            full = (T - 1) * P

            def load_w():
                sp.dma_start(w13[:, :, 0:DA], W1.rearrange("(c p) a -> p c a", p=P)).then_inc(w_in, 16)
                sp.dma_start(w13[:, :, DA:2 * DA], W3.rearrange("(c p) a -> p c a", p=P)).then_inc(w_in, 16)
                sp.dma_start(w2[:, 0:DA], W2).then_inc(w_in, 16)

            sp.wait_ge(consts_made, 1)
            for k, tiles_of in enumerate(x_chunks):
                a, b = tiles_of[0], tiles_of[-1] + 1
                sp.dma_start(XBf[:, a:b, :], x[a * P:b * P, :].rearrange("(t p) d -> p t d", p=P)).then_inc(x_in[k], 16)
                if k == 0:
                    load_w()
            sp.dma_start(XBf[0:TAIL, T - 1, :], x[full:N, :]).then_inc(x_in[2], 16)
            sp.dma_start(U1[:, :, :], U1_0.rearrange("(c p) a -> p c a", p=P)).then_inc(U_in, 16)
            sp.dma_start(U2[:, :, :], U2_0.rearrange("(c p) a -> p c a", p=P)).then_inc(U_in, 16)
            sp.dma_start(AD[:, 0:N], adj[0:P, :]).then_inc(adj_in, 16)

            def store_qk(s, i, n, par, qk_parts):
                sp.wait_ge(parts_made, n + 3)
                q_rows = q_dram[s, bass.ds(i, 1), :, :].rearrange("o r c -> (o r) c")
                sp.dma_start(q_rows[0:DA, :], qk_parts[0:DA, :, :].rearrange("r a c -> r (a c)")).then_inc(qk_stored[par], 16)
                sp.dma_start(q_rows[DA:P, 0:2 * P], qk_parts[0:DA, 0:2, :].rearrange("r a c -> r (a c)")).then_inc(qk_stored[par], 16)
                sp.dma_start(q_rows[DA:P, 2 * P:3 * P], qk_parts[0:DA, 0, :]).then_inc(qk_stored[par], 16)
                sp.dma_start(k_dram[s, :, :, bass.ds(i * P, P)], qk_parts[DA:P, :, :]).then_inc(qk_stored[par], 16)

            def store_h(i, par):
                sp.wait_ge(h_made, i + 1)
                sp.dma_start(h_plus_z[bass.ds(i, 1), :, :].rearrange("o p d -> (o p) d"), XN[par][:, :]).then_inc(h_stored[par], 16)

            def phase0(i, j, par, last):
                if not last:
                    store_h(i + 1, 1 - par)
                store_qk(0, i, i, par, stage[par][3])

            store_h(0, 0)
            tiles(sp, phase0)
            for par in range(2):
                sp.wait_ge(h_stored[par], 16 * (T // 2))

            def load_q(s, i, par):
                sp.dma_start(qs[par][:, :, :].rearrange("r a c -> r (a c)"),
                             q_dram[s, bass.ds(i, 1), :, :].rearrange("o r c -> (o r) c")).then_inc(q_in[par], 16)

            def tile(s, i, j, par, last, last_pair):
                g = s * T + i
                if not last_pair:
                    sp.wait_ge(logits_made, (g + 1) * NCH)
                    load_q(s, i + 2, par)
                if s == 0:
                    sp.wait_ge(z_stored, 16 * (i + 1))
                else:
                    sp.wait_ge(y_done, i + 1)
                sp.dma_start(zt[:, :], h_plus_z[bass.ds(i, 1), :, :].rearrange("o p d -> (o p) d")).then_inc(z_in, 16)
                if s == 1:
                    sp.wait_ge(out_stored, 16 * (i + 1))
                    if last:
                        sp.dma_start(x_rows[0:TAIL, :], x[full:N, :]).then_inc(x_rows_in, 16)
                    else:
                        sp.dma_start(x_rows[:, :], x[bass.ds(i * P, P), :]).then_inc(x_rows_in, 16)
                if s == 0:
                    for k, bl in enumerate(blocks):
                        if k == 1:
                            sp.wait_ge(lo_made, T + 2 * i + 1)
                            sp.dma_start(xa_next[bass.ds(i, 1), :, :].rearrange("o p d -> (o p) d"), xah[:, :]).then_inc(xa_stored, 16)
                        if k == min(4, NG - 1):
                            store_qk(1, i, T + i, par, qk_parts)
                        n, slot, _, _ = group(s, i, par, NG + k)
                        sp.wait_ge(lo_left, n + 3)
                        sp.dma_start(rt_dram[bass.ds(i, 1), :, bl[0]:bl[-1] + 1, :].rearrange("o p b c -> (o p) b c"),
                                     ring[slot][:, 0:len(bl), :]).then_inc(slot_stored[slot], 16)
                    if not last:
                        sp.wait_ge(turned, group(s, i, par, 2 * NG - 1)[0] + 1)
                        if last_pair:
                            sp.dma_start(AD[0:TAIL, 0:N], adj[full:N, :]).then_inc(adj_in, 16)
                        else:
                            sp.dma_start(AD[:, 0:N], adj[bass.ds((i + 1) * P, P), :]).then_inc(adj_in, 16)
                elif not last:
                    sp.wait_ge(RT_used, i + 1)
                    sp.dma_start(RT, rt_dram[bass.ds(i + 1, 1), :, :, :].rearrange("o p b c -> (o p) b c")).then_inc(rt_in, 16)
                if s == 0:
                    sp.wait_ge(z_taken, i + 2)
                    sp.dma_start(h_plus_z[bass.ds(i, 1), :, :].rearrange("o p d -> (o p) d"), zt[:, :]).then_inc(z_stored, 16)
                else:
                    sp.wait_ge(y_done, i + 2)
                    if last:
                        sp.dma_start(out[full:N, :], x_rows[0:TAIL, :]).then_inc(out_stored, 16)
                    else:
                        sp.dma_start(out[bass.ds(i * P, P), :], x_rows[:, :]).then_inc(out_stored, 16)

            for s in range(2):
                for par in range(2):
                    sp.wait_ge(qk_stored[par], 64 * (PAIRS * (s + 1) + 1))
                for rows, part, K in ((0, 0, K12), (DA, 1, K12), (0, 0, K13), (DA, 2, K13)):
                    sp.dma_start(K[rows:rows + DA, :], k_dram[s, :, part, :]).then_inc(k_in, 16)
                for par in range(2):
                    if s == 1:
                        sp.wait_ge(logits_made, (T - 1 + par) * NCH)
                    load_q(s, par, par)
                if s == 1:
                    sp.wait_ge(xa_stored, 16 * (T + 1))
                    sp.wait_ge(z_stored, 16 * (T + 1))
                    sp.dma_start(gamma_rows, gamma.partition_broadcast(P)).then_inc(gb_in, 16)
                    sp.dma_start(beta_rows, beta.partition_broadcast(P)).then_inc(gb_in, 16)
                    sp.wait_ge(used, T * L[0] + RING)
                    for slot in range(RING):
                        sp.wait_ge(slot_stored[slot], 16 * (T * stores_of(slot) + 1))
                    for half in range(2):
                        a, b = half * T // 2, (half + 1) * T // 2
                        sp.dma_start(XA[:, a:b, :], xa_next[a:b, :, :].rearrange("t p d -> p t d")).then_inc(xa_in, 16)
                    sp.dma_start(RT, rt_dram[0, :, :, :]).then_inc(rt_in, 16)
                    sp.wait_ge(z_added, 2 * T + 1)
                    sp.dma_start(U1[:, :, :], U1_1.rearrange("(c p) a -> p c a", p=P)).then_inc(U_in, 16)
                    sp.dma_start(U2[:, :, :], U2_1.rearrange("(c p) a -> p c a", p=P)).then_inc(U_in, 16)
                with sp.Fori(0, T // 2 - 1) as j:
                    tile(s, j * 2, j, 0, False, False)
                    tile(s, j * 2 + 1, j, 1, False, False)
                tile(s, T - 2, T // 2 - 1, 0, False, True)
                tile(s, T - 1, T // 2 - 1, 1, True, True)

            sp.wait_ge(out_stored, 16 * (T + 1))

        @block.gpsimd
        def _(pool):
            nc.gpsimd.memset(ident[:, :], 0.0).then_inc(ident_made, 1)
            pool.wait_ge(ident_made, 1)
            nc.gpsimd.affine_select(out=ident[:, :], in_=ident[:, :], compare_op=ALU.not_equal, fill=1.0, base=0,
                                    pattern=[[-1, P]], channel_multiplier=1).then_inc(ident_made, 1)
            pool.wait_ge(ident_made, 2)
            nc.gpsimd.tensor_scalar(minus_eye[:, :], ident[:, :], -1.0, 0.0, ALU.mult, ALU.add).then_inc(ident_made, 1)

            def make_parts(n, st):
                _, _, qk, qk_parts = stage[st]
                pool.wait_ge(q2_taken, n + 3)
                nc.gpsimd.tensor_tensor(qk[:, :], qk[:, :], qk_parts[:, 0, :], ALU.subtract)
                pool.drain()
                nc.gpsimd.tensor_copy(qk_parts[:, 1, :], qk[:, :])
                pool.drain()
                nc.gpsimd.tensor_tensor(qk_parts[:, 2, :], qk[:, :], qk_parts[:, 1, :], ALU.subtract).then_inc(parts_made, 1)

            def lo_of_h(i, par):
                pool.wait_ge(h_made, i + 1)
                pool.wait_ge(h_hi, i + 1)
                nc.gpsimd.tensor_tensor(XA[:, bass.ds(i, 1), D:2 * D].rearrange("p o d -> p (o d)"), XN[par][:, :],
                                        XA[:, bass.ds(i, 1), 0:D].rearrange("p o d -> p (o d)"),
                                        ALU.subtract).then_inc(lo_made, 1)

            def phase0(i, j, par, last):
                if not last:
                    lo_of_h(i + 1, 1 - par)
                make_parts(i, par)

            lo_of_h(0, 0)
            tiles(pool, phase0)

            def add_eye(i):
                pool.wait_ge(adj_in, 16 * (i + 1))
                blk = AD[:, bass.ds(i * P, P)]
                nc.gpsimd.tensor_tensor(blk, blk, ident[:, :], ALU.add).then_inc(adj_eye, 1)

            def tile0(i, j, par, last):
                add_eye(i)
                pool.wait_ge(xnA_made, i + 2)
                nc.gpsimd.tensor_tensor(xah[:, D:2 * D], XN[1][:, :], xah[:, 0:D], ALU.subtract).then_inc(lo_made, 1)
                make_parts(T + i, OWN)
                pool.wait_ge(xnR_made, i + 2)
                nc.gpsimd.tensor_tensor(XB[:, bass.ds(i, 1), D:2 * D].rearrange("p o d -> p (o d)"), XN[0][:, :],
                                        XB[:, bass.ds(i, 1), 0:D].rearrange("p o d -> p (o d)"),
                                        ALU.subtract).then_inc(lo_made, 1)

            tiles(pool, tile0)

            def move_t(i, par):
                for k in range(LEVELS):
                    step_up = ratio(k + 1)
                    pool.wait_ge(sums_made, (i - 1) * LEVELS + k + 1)
                    nc.gpsimd.tensor_tensor(pool_mass, signs[par], t_of[par], ALU.mult)
                    if k == 0:
                        nc.gpsimd.tensor_tensor(pool_goal, S_part[par][0], S_part[par][1], ALU.add)
                        pool.drain()
                        nc.gpsimd.tensor_scalar(pool_goal, pool_goal, P_TOP, 0.0, ALU.mult, ALU.add)
                    pool.drain()
                    nc.gpsimd.tensor_scalar(pool_mass, pool_mass, 0.5, above_t[par], ALU.mult, ALU.add)
                    pool.drain()
                    nc.gpsimd.tensor_scalar(pool_mass, t_of[par], N / 2, pool_mass, ALU.mult, ALU.add)
                    pool.drain()
                    nc.gpsimd.tensor_scalar(pool_up, pool_mass, pool_goal, step_up - 1 / step_up, ALU.is_ge, ALU.mult)
                    pool.drain()
                    nc.gpsimd.tensor_scalar(t_of[par], pool_up, 1 / step_up, t_of[par], ALU.add, ALU.mult)
                    pool.drain()
                    nc.gpsimd.tensor_scalar(minus_t[par], t_of[par], -1.0, 0.0, ALU.mult, ALU.add).then_inc(t_moved, 1)

            def finish(i):
                ops = nc.gpsimd
                pool.wait_ge(x_rows_in, 16 * (i + 1))
                ops.tensor_tensor(x_rows, x_rows, beta_rows, ALU.add)
                pool.wait_ge(stats_made, T + i + 1)
                ops.tensor_tensor(var_y, moments[:, 1:2], col["eps_y"], ALU.add)
                pool.drain()
                ops.tensor_copy(seed_y, var_y.bitcast(i32))
                pool.drain()
                ops.tensor_scalar(root_y.bitcast(i32), seed_y, -0.5, float(0x5F3759DF), ALU.mult, ALU.add)
                ops.tensor_scalar(var_y, var_y, -0.5, 0.0, ALU.mult, ALU.add)
                pool.drain()
                for _ in range(4):
                    ops.tensor_tensor(tmp_y, root_y, root_y, ALU.mult)
                    pool.drain()
                    ops.tensor_scalar(tmp_y, tmp_y, var_y, 1.5, ALU.mult, ALU.add)
                    pool.drain()
                    ops.tensor_tensor(root_y, root_y, tmp_y, ALU.mult)
                    pool.drain()
                ops.tensor_scalar(zt[:, :], zt[:, :], moments[:, 0:1], root_y, ALU.subtract, ALU.mult)
                pool.drain()
                ops.tensor_tensor(zt[:, :], zt[:, :], gamma_rows, ALU.mult)
                pool.drain()
                ops.tensor_tensor(x_rows, zt[:, :], x_rows, ALU.add).then_inc(y_done, 1)

            move_t(1, 1)
            pool.wait_ge(gb_in, 32)
            with pool.Fori(0, T // 2 - 1) as j:
                move_t(j * 2 + 2, 0)
                finish(j * 2)
                move_t(j * 2 + 3, 1)
                finish(j * 2 + 1)

            finish(T - 2)
            finish(T - 1)

        @block.scalar
        def _(act):
            def root(i):
                act.wait_ge(stats_made, i + 1)
                nc.scalar.activation(rstd[:, bass.ds(i, 1)], mv[:, bass.ds(i, 1), 1], ACT.Sqrt, bias=col["eps"]).then_inc(root_made, 1)

            def take_xT(n, st=OWN):
                act.wait_ge(x_turned, n + 1)
                nc.scalar.activation(stage[st][0][:, :, :], stage_ps[st][:, :, :], ACT.Copy).then_inc(xT_made, 1)

            def take_qk(n, par, st=OWN):
                _, qf, qk, qk_parts = stage[st]
                pX = stage_ps[st]
                act.wait_ge(qk_made, n + 3)
                if st == OWN:
                    act.wait_ge(parts_made, n + 2)
                else:
                    act.wait_ge(parts_made, n + 1)
                nc.scalar.activation(qf, pX[0:DA, 0, :], ACT.Copy)
                nc.scalar.activation(qk[DA:2 * DA, :], pX[DA:2 * DA, 0, :], ACT.Copy)
                if st == OWN:
                    act.wait_ge(qk_stored[1 - par], (n - T + par) * 32 + 64 * (PAIRS + 1))
                else:
                    act.wait_ge(qk_stored[par], (n - par) * 32 + 64)
                nc.scalar.activation(qk_parts[DA:2 * DA, 0, :], pX[DA:2 * DA, 0, :], ACT.Copy).then_inc(qf_made, 1)
                act.wait_ge(q2_made, n + 1)
                nc.scalar.activation(qk_parts[0:DA, 0, :], pX[0:DA, 1, :], ACT.Copy)
                nc.scalar.activation(qk[0:DA, :], pX[0:DA, 1, :], ACT.Copy).then_inc(q2_taken, 1)

            def take_h(i, par):
                act.wait_ge(h_made, i + 1)
                nc.scalar.activation(XA[:, bass.ds(i, 1), 0:D].rearrange("p o d -> p (o d)"), XN[par][:, :], ACT.Copy).then_inc(h_hi, 1)
                act.wait_ge(qk_made, i + 1)
                take_xT(i, par)

            def phase0(i, j, par, last):
                if not isinstance(i, int):
                    root(i + 2)
                if not last:
                    take_h(i + 1, 1 - par)
                take_qk(i, par, par)

            root(0)
            root(1)
            take_h(0, 0)
            tiles(act, phase0)

            halves = (slice(0, HALF), slice(HALF, N))

            def exp(s, i, par, h):
                if h == 0:
                    act.wait_ge(max_made, s * T + i + 1)
                e = E[par][:, halves[h]]
                nc.scalar.activation(e, e, ACT.Exp, bias=nb[par], scale=1.0 / FS ** 2,
                                     accum_out=S_part[par][h]).then_inc(exp_made, 1)

            def adj_sum(i, h):
                if h == 0:
                    act.wait_ge(adj_eye, i + 1)
                a = AD[:, halves[h]]
                nc.scalar.activation(a, a, ACT.Copy, accum_out=adj_part[h]).then_inc(adj_summed, 1)

            def adj_scale(i, h):
                if h == 0:
                    act.wait_ge(adj_recip, i + 1)
                a = AD[:, halves[h]]
                nc.scalar.activation(a, a, ACT.Copy, scale=col["row_scale"]).then_inc(adj_scaled, 1)

            def level(i, par, k):
                if k == 0:
                    act.wait_ge(exp_made, 2 * (T + i + 1))
                else:
                    act.wait_ge(t_moved, (i - 1) * LEVELS + k)
                nc.scalar.activation(unread[:, :], E[par][:, 0:N], ACT.Relu, bias=minus_t[par], accum_out=above_t[par])
                act.drain()
                nc.scalar.activation(unread[:, :], E[par][:, 0:N], ACT.Sign, bias=minus_t[par],
                                     accum_out=signs[par]).then_inc(sums_made, 1)

            def hi_part(s, i, j, par, q):
                n, slot, bank, free = group(s, i, par, q)
                act.wait_ge(turned, n + 1)
                act.wait_ge(used, free + RING)
                if s == 0:
                    act.wait_ge(slot_stored[slot], 16 * (i * stores_of(slot) + stores_of(slot, q) + 1))
                m = len(blocks[q % NG])
                nc.scalar.activation(ring[slot][:, 0:m, 0:P], pT[bank][:, 0:m, :], ACT.Copy).then_inc(hi_made, 1)

            def lo_part(s, i, j, par, q):
                n, slot, bank, _ = group(s, i, par, q)
                act.wait_ge(hi_taken, n + 1)
                m = len(blocks[q % NG])
                nc.scalar.activation(ring[slot][:, 0:m, P:2 * P], pT[bank][:, 0:m, :], ACT.Copy).then_inc(lo_left, 1)

            def new_rows_of_Xa(s, i, par):
                g = s * T + i
                act.wait_ge(used, group(s, i, par, NG - 1)[0] + 1 + RING)
                act.wait_ge(x_turned, T + 2 * g)
                if s == 0:
                    act.wait_ge(xa_stored, 16 * (i + 1))
                    act.wait_ge(lo_made, T + 2 * i)
                    nc.scalar.activation(xah[:, 0:D], pA[:, :], ACT.Copy, scale=rinv[par])
                nc.scalar.activation(XN[1][:, :], pA[:, :], ACT.Copy, scale=rinv[par]).then_inc(xnA_made, 1)

            def new_rows_of_Xf(s, i, par):
                g = s * T + i
                if s == 0:
                    act.wait_ge(used, group(s, i, par, 2 * NG - 1)[0] + 1 + RING)
                    act.wait_ge(lo_made, T + 2 * i)
                    nc.scalar.activation(XB[:, bass.ds(i, 1), 0:D].rearrange("p o d -> p (o d)"), pR[:, :], ACT.Copy,
                                         scale=1.0 / RSC)
                else:
                    act.wait_ge(RT_used, i + 1)
                act.wait_ge(x_turned, T + 2 * g)
                nc.scalar.activation(XN[0][:, :], pR[:, :], ACT.Copy, scale=1.0 / RSC).then_inc(xnR_made, 1)

            def tile(s, i, j, par, first):
                g = s * T + i
                more = has_more(i)
                for q in range(L[s] + 1):
                    if q < L[s]:
                        hi_part(s, i, j, par, q)
                    if q >= 1:
                        lo_part(s, i, j, par, q - 1)
                    if s == 0:
                        if q == 0 and not first:
                            new_rows_of_Xf(0, i - 1, 1 - par)
                        if q == 1 and not first:
                            take_xT_of_Xf(i - 1)
                        if q - SUM_AT in (0, 1):
                            adj_sum(i, q - SUM_AT)
                        if q in (NG - 2, NG - 1):
                            adj_scale(i, q - (NG - 2))
                        if q == NG + 1:
                            new_rows_of_Xa(s, i, par)
                        if q == NG + 2:
                            act.wait_ge(z_added, 2 * g + 1)
                            take_xT(T + 2 * g)
                        if q == NG + 3:
                            take_qk(T + i, par)
                        if q in (2 * NG - 1, 2 * NG) and more:
                            exp(s, i + 2, par, q - (2 * NG - 1))
                if s == 1:
                    new_rows_of_Xa(s, i, par)
                    act.wait_ge(z_added, 2 * g + 1)
                    take_xT(T + 2 * g)
                    if more:
                        exp(s, i + 2, par, 0)
                        exp(s, i + 2, par, 1)
                        for k in range(LEVELS // 2):
                            level(i + 2, par, k)
                    new_rows_of_Xf(s, i, par)
                    act.wait_ge(z_added, 2 * g + 2)
                    take_xT(T + 2 * g + 1)
                    if more:
                        for k in range(LEVELS // 2, LEVELS):
                            level(i + 2, par, k)

            def take_xT_of_Xf(i):
                act.wait_ge(z_added, 2 * i + 1 + 1)
                act.wait_ge(qk_made, T + i + 3)
                take_xT(T + 2 * i + 1)

            for s in range(2):
                if s == 1:
                    for slot in range(RING):
                        act.wait_ge(slot_stored[slot], 16 * (T * stores_of(slot) + 1))
                for par in range(2):
                    for h in range(2):
                        exp(s, par, par, h)
                if s == 1:
                    for k in range(LEVELS):
                        level(1, 1, k)
                if s == 0:
                    tiles_after_first(act, lambda i, j, par, first: tile(0, i, j, par, first))
                    new_rows_of_Xf(0, T - 1, 1)
                    take_xT_of_Xf(T - 1)
                else:
                    tiles(act, lambda i, j, par, last: tile(1, i, j, par, False))

        @block.vector
        def _(dve):
            nc.vector.memset(w2, 0.0)
            nc.vector.memset(XBf[:, T - 1, :], 0.0)
            dve.drain().then_inc(consts_made, 1)
            for k in range(ALL_PASSES):
                nc.vector.memset(halving[:, k:k + 1], ratio(k, WHOLE_SPAN))
            nc.vector.memset(flags[:, :], 0.0)
            nc.vector.memset(col["eps"], EPS)
            nc.vector.memset(col["eps_y"], EPS * FS ** 2)
            nc.vector.memset(E[0][:, N:NP], 0.0)
            nc.vector.memset(E[1][:, N:NP], 0.0)
            nc.vector.memset(AD[:, N:NP], 0.0)
            dve.drain()
            for free, n in ((logits_taken, 2), (lo_left, 2), (used, RING), (parts_made, 2), (qk_made, 2), (q2_taken, 2),
                            *((x, 16) for x in slot_stored), (xnR_made, 1), (xnA_made, 1), (z_added, 1), (z_taken, 1), (z_stored, 16),
                            (xa_stored, 16), (qk_stored[0], 64), (qk_stored[1], 64), (y_done, 1), (out_stored, 16)):
                dve.sem_inc(free, n)

            def mean_and_variance(src):
                nc.vector.bn_stats(st6, src)
                dve.drain()
                nc.vector.bn_aggr(moments, st6)
                dve.drain()

            def stats(i, src):
                mean_and_variance(src)
                nc.vector.tensor_copy(mv[:, bass.ds(i, 1), :].rearrange("p o c -> p (o c)"), moments)

            def stats_of_x(i):
                stats(i, XBf[:, bass.ds(i, 1), :].rearrange("p o d -> p (o d)"))
                dve.drain().then_inc(stats_made, 1)

            def phase0(i, j, par, more=True, first=False):
                if more:
                    stats_of_x(i + 2)
                xi = XBf[:, bass.ds(i, 1), :].rearrange("p o d -> p (o d)")
                dve.wait_ge(root_made, i + 1)
                nc.vector.reciprocal(rstd[:, bass.ds(i, 1)], rstd[:, bass.ds(i, 1)])
                dve.drain()
                nc.vector.tensor_scalar(xi, xi, mv[:, bass.ds(i, 1), 0], rstd[:, bass.ds(i, 1)], ALU.subtract, ALU.mult)
                dve.drain()
                if not first:
                    dve.wait_ge(x_turned, i - 1)
                    dve.wait_ge(h_hi, i - 1)
                    dve.wait_ge(lo_made, i - 1)
                    dve.wait_ge(h_stored[par], 16 * j)
                nc.vector.tensor_scalar(XN[par][:, :], xi, 0.0, FS, ALU.max, ALU.mult).then_inc(h_made, 1)

            dve.wait_ge(x_in[0], 16)
            stats_of_x(0)
            stats_of_x(1)
            phase0(0, 0, 0, first=True)
            phase0(1, 0, 1, first=True)
            dve.wait_ge(x_in[1], 16)
            with dve.Fori(1, J1) as j:
                phase0(j * 2, j, 0)
                phase0(j * 2 + 1, j, 1)
            dve.wait_ge(x_in[2], 32)
            with dve.Fori(J1, PAIRS - 1) as j:
                phase0(j * 2, j, 0)
                phase0(j * 2 + 1, j, 1)
            phase0(T - 2, PAIRS - 1, 0, more=False)
            phase0(T - 1, PAIRS - 1, 1, more=False)

            def take_logits(s, i, par):
                g = s * T + i
                if not isinstance(i, int) or i >= 2:
                    dve.wait_ge(turned, group(s, i - 2, par, NG - 1)[0] + 1)
                elif s == 1:
                    dve.wait_ge(turned, T * L[0])
                for c in range(NCH):
                    w = min(CHUNK, N - c * CHUNK)
                    dve.wait_ge(logits_made, g * NCH + c + 1)
                    nc.vector.tensor_scalar(E[par][:, c * CHUNK:c * CHUNK + w], pL[(par + c) % 2][:, 0:w], 1.0, None,
                                            ALU.mult, ALU.max, accum_out=mx8[:, c:c + 1]).then_inc(logits_taken, 1)
                dve.drain()
                nc.vector.tensor_reduce(col["neg_max"], mx8, AX.X, ALU.max)
                dve.drain()
                if s == 1:
                    nc.vector.memset(t_of[par], BOTTOM * ratio(0))
                    nc.vector.memset(minus_t[par], -BOTTOM * ratio(0))
                nc.vector.tensor_scalar(nb[par], col["neg_max"], -1.0 / FS ** 2, math.log(RSC), ALU.mult, ALU.add).then_inc(max_made, 1)

            def light_pass(par, k):
                c, step_up = col, ratio(k + 1)
                nc.vector.scalar_tensor_tensor(out=choice[:, 0:N], in0=E[par][:, 0:N], scalar=c["t"], in1=E[par][:, 0:N],
                                               op0=ALU.is_gt, op1=ALU.mult, accum_out=c["mass"])
                dve.drain()
                nc.vector.tensor_scalar(c["up"], c["mass"], c["goal"], step_up - 1 / step_up, ALU.is_ge, ALU.mult)
                dve.drain()
                nc.vector.scalar_tensor_tensor(out=c["t"], in0=c["up"], scalar=1 / step_up, in1=c["t"], op0=ALU.add, op1=ALU.mult)
                dve.drain()

            def full_pass(par):
                c = col
                nc.vector.scalar_tensor_tensor(out=choice[:, 0:N], in0=E[par][:, 0:N], scalar=c["t"], in1=E[par][:, 0:N],
                                               op0=ALU.is_gt, op1=ALU.mult, accum_out=c["mass"])
                dve.drain()
                nc.vector.tensor_scalar(c["up"], c["mass"], c["goal"], None, ALU.is_ge)
                dve.drain()
                nc.vector.scalar_tensor_tensor(out=c["lo"], in0=c["up"], scalar=c["t"], in1=c["lo"], op0=ALU.mult, op1=ALU.max)
                nc.vector.scalar_tensor_tensor(out=c["far"], in0=c["up"], scalar=BIG, in1=c["t"], op0=ALU.mult, op1=ALU.add)
                dve.drain()
                nc.vector.tensor_tensor(c["hi"], c["hi"], c["far"], ALU.min)
                dve.drain()

            def eight_below(par):
                c, e = col, E[par]
                for h, (a, b) in enumerate(((0, HALF), (HALF, N))):
                    nc.vector.scalar_tensor_tensor(out=masked[:, 0:b - a], in0=e[:, a:b], scalar=c["hi"], in1=e[:, a:b],
                                                   op0=ALU.is_le, op1=ALU.mult, accum_out=c["tmp"] if h == 0 else c["tmp2"])
                    dve.drain()
                    nc.vector.max(v16[:, 8 * h:8 * h + 8], masked[:, 0:b - a])
                    dve.drain()
                nc.vector.max(v8, v16)
                nc.vector.tensor_tensor(c["mass_hi"], c["tmp"], c["tmp2"], ALU.add)
                dve.drain()
                nc.vector.tensor_tensor(c["mass_hi"], S[par], c["mass_hi"], ALU.subtract)
                dve.drain()

            def threshold(par):
                c = col
                nc.vector.tensor_tensor_scan(cum8, v8, v8, c["mass_hi"], ALU.add, ALU.max)
                dve.drain()
                nc.vector.tensor_scalar(w8, cum8, c["goal"], None, ALU.is_ge)
                dve.drain()
                nc.vector.tensor_tensor(cum8, w8, v8, ALU.mult)
                dve.drain()
                nc.vector.tensor_reduce(c["tmp"], cum8, AX.X, ALU.max)
                dve.drain()
                nc.vector.tensor_tensor(c["v_star"], c["tmp"], v8[:, 7:8], ALU.max)
                dve.drain()
                nc.vector.scalar_tensor_tensor(out=cum8, in0=v8, scalar=c["v_star"], in1=v8, op0=ALU.is_gt, op1=ALU.mult,
                                               accum_out=c["v_more"])
                dve.drain()
                nc.vector.tensor_tensor(c["mass_gt"], c["mass_hi"], c["v_more"], ALU.add)
                dve.drain()

            def flag_plain():
                c = col
                nc.vector.tensor_reduce(c["tmp"], w8, AX.X, ALU.add)
                nc.vector.tensor_scalar(cum8, v8, c["v_star"], 0.0, ALU.is_ge, ALU.add, accum_out=c["tmp2"])
                dve.drain()
                nc.vector.tensor_tensor(c["up"], c["tmp"], c["tmp2"], ALU.add)
                nc.vector.tensor_scalar(c["far"], c["tmp"], 2.0, None, ALU.is_lt)
                dve.drain()
                nc.vector.scalar_tensor_tensor(out=flags[:, 0:1], in0=c["up"], scalar=9.0, in1=c["far"],
                                               op0=ALU.not_equal, op1=ALU.max)
                dve.drain()

            def count_equals(par):
                c, n = col, count[:, 0:N]
                nc.vector.tensor_scalar(n, E[par][:, 0:N], c["v_star"], None, ALU.is_equal)
                dve.drain()
                nc.vector.tensor_tensor_scan(n, n, n, 0.0, ALU.add, ALU.max)
                dve.drain()
                nc.vector.scalar_tensor_tensor(out=c["reach"], in0=count[:, N - 1:N], scalar=c["v_star"], in1=c["mass_gt"],
                                               op0=ALU.mult, op1=ALU.add)
                dve.drain()
                nc.vector.tensor_scalar(c["tmp"], c["reach"], 1 + SLACK, c["goal"], ALU.mult, ALU.is_lt)
                nc.vector.tensor_scalar(c["tmp2"], c["mass_gt"], 1 - SLACK, c["goal"], ALU.mult, ALU.is_ge)
                dve.drain()
                nc.vector.tensor_tensor(flags[:, 0:1], c["tmp"], c["tmp2"], ALU.max)
                dve.drain()

            def any_flag():
                c = col
                nc.vector.transpose(flagsT[:, :], flags[:, :])
                dve.drain()
                nc.vector.tensor_reduce(c["bad"], flagsT[:, :], AX.X, ALU.max)
                dve.drain()
                for q in range(4):
                    nc.vector.tensor_copy(w8[0:1, q:q + 1], c["bad"][32 * q:32 * q + 1, :])
                dve.drain()
                nc.vector.tensor_reduce(flag_i[0:1, :], w8[0:1, 0:4], AX.X, ALU.max)
                dve.drain()
                return dve.value_load(flag_i[0:1, 0:1], min_val=0, max_val=1)

            def peel(par):
                c = col
                nc.vector.tensor_scalar(c["up"], c["reach"], c["goal"], None, ALU.is_ge)
                nc.vector.tensor_scalar(c["below"], c["v_star"], 1.0 - 2.0 ** -24, None, ALU.mult)
                dve.drain()
                nc.vector.scalar_tensor_tensor(out=c["tmp"], in0=c["up"], scalar=BIG, in1=c["below"], op0=ALU.mult, op1=ALU.add)
                dve.drain()
                nc.vector.tensor_tensor(c["hi"], c["hi"], c["tmp"], ALU.min)
                dve.drain()
                eight_below(par)
                threshold(par)
                count_equals(par)

            def search_all(par):
                c = col
                nc.vector.memset(c["lo"], LEAST)
                nc.vector.memset(c["hi"], TOP)
                dve.drain()
                with dve.Fori(0, ALL_PASSES) as k:
                    nc.vector.tensor_tensor(c["t"], c["lo"], halving[:, bass.ds(k, 1)], ALU.mult)
                    dve.drain()
                    full_pass(par)
                eight_below(par)
                threshold(par)
                count_equals(par)

            def keep_by_count(par):
                c = col
                e, flagged = E[par][:, 0:N], choice[:, 0:N]
                count_equals(par)
                with dve.If(any_flag() != 0):
                    peel(par)
                    with dve.If(any_flag() != 0):
                        search_all(par)
                    with dve.Else():
                        dve.drain()
                    dve.drain()
                with dve.Else():
                    dve.drain()
                nc.vector.tensor_tensor(c["tmp"], c["goal"], c["mass_gt"], ALU.subtract)
                nc.vector.reciprocal(c["tmp2"], c["v_star"])
                nc.vector.tensor_scalar(c["below"], c["v_star"], 1.0 - 2.0 ** -24, None, ALU.mult)
                dve.drain()
                nc.vector.tensor_scalar(c["quota"], c["tmp"], c["tmp2"], 1.0, ALU.mult, ALU.add)
                nc.vector.tensor_tensor(c["gap"], c["v_star"], c["below"], ALU.subtract)
                dve.drain()
                nc.vector.tensor_scalar(flagged, count[:, 0:N], c["quota"], c["gap"], ALU.is_ge, ALU.mult)
                dve.drain()
                nc.vector.scalar_tensor_tensor(out=flagged, in0=flagged, scalar=c["below"], in1=e, op0=ALU.add, op1=ALU.is_lt)
                dve.drain()
                nc.vector.scalar_tensor_tensor(out=e, in0=flagged, scalar=1.0, in1=e, op0=ALU.mult, op1=ALU.mult,
                                               accum_out=c["kept"])
                dve.drain()

            def search(s, i, par, between, first=0):
                c, e = col, E[par][:, 0:N]
                dve.wait_ge(exp_made, 2 * (s * T + i + 1))
                nc.vector.tensor_tensor(S[par], S_part[par][0], S_part[par][1], ALU.add)
                if first == 0:
                    nc.vector.memset(c["t"], BOTTOM * ratio(0))
                else:
                    dve.wait_ge(t_moved, i * LEVELS)
                    nc.vector.tensor_scalar(c["t"], t_of[par], 1.0, None, ALU.mult)
                dve.drain()
                nc.vector.tensor_scalar(c["goal"], S[par], P_TOP, None, ALU.mult)
                dve.drain()
                for k in range(first, PASSES[s]):
                    light_pass(par, k)
                    between(k)
                nc.vector.tensor_scalar(c["hi"], c["t"], ratio(PASSES[s]) * (1 + 1e-6), None, ALU.mult)
                dve.drain()
                eight_below(par)
                threshold(par)
                if s == 1:
                    keep_by_count(par)
                else:
                    flag_plain()
                    with dve.If(any_flag() != 0):
                        keep_by_count(par)
                    with dve.Else():
                        nc.vector.scalar_tensor_tensor(out=e, in0=e, scalar=c["v_star"], in1=e, op0=ALU.is_ge, op1=ALU.mult,
                                                       accum_out=c["kept"])
                        dve.drain()
                nc.vector.reciprocal(rinv[par], c["kept"]).then_inc(mask_made, 1)

            def adj_recip_of(i):
                dve.wait_ge(adj_summed, 2 * (i + 1))
                nc.vector.tensor_tensor(col["row_sum"], adj_part[0], adj_part[1], ALU.add)
                dve.drain()
                nc.vector.tensor_scalar(col["row_sum"], col["row_sum"], 1e-12, 1.0 / RSC, ALU.max, ALU.mult)
                dve.drain()
                nc.vector.reciprocal(col["row_scale"], col["row_sum"]).then_inc(adj_recip, 1)

            def take_Z(s, i):
                g = s * T + i
                dve.wait_ge(z_in, 16 * (g + 1))
                dve.wait_ge(z_added, 2 * (g + 1) + 1)
                nc.vector.tensor_tensor(zt[:, :], pZ[:, :], zt[:, :], ALU.add)
                dve.drain().then_inc(z_taken, 1)

            def tile0(i, par, first, last):
                def between(k):
                    if k == 1 and not first:
                        take_Z(0, i - 1)
                    if k == 2:
                        adj_recip_of(i)
                    if k == TAKE[0] and has_more(i):
                        take_logits(0, i + 2, par)

                if last:
                    adj_recip_of(i)
                    take_Z(0, i - 1)
                    take_Z(0, i)
                else:
                    search(0, i + 1, 1 - par, between)

            def tile1(i, par, last):
                def between(k):
                    if k == TAKE[1] and has_more(i):
                        take_logits(1, i + 2, par)

                if not last:
                    search(1, i + 1, 1 - par, between, LEVELS)
                take_Z(1, i)
                mean_and_variance(zt[:, :])
                dve.sem_inc(stats_made, 1)

            for s in range(2):
                take_logits(s, 0, 0)
                take_logits(s, 1, 1)
                search(s, 0, 0, lambda k: None)
                if s == 0:
                    tiles_after_first(dve, lambda i, j, par, first: tile0(i, par, first, isinstance(i, int) and i == T - 1))
                else:
                    tiles(dve, lambda i, j, par, last: tile1(i, par, last))

        @block.tensor
        def _(pe):
            pe.wait_ge(ident_made, 3)
            pe.wait_ge(w_in, 16 * 3)

            def turn_x(rows, st=OWN):
                pX = stage_ps[st]
                for c in range(DC):
                    last = nc.tensor.transpose(pX[:, c, :], rows[:, c * P:(c + 1) * P], ident[:, :])
                last.then_inc(x_turned, 1)

            def add_z(n, U, first):
                pe.wait_ge(xT_made, n + 1)
                for c in range(DC):
                    last = nc.tensor.matmul(pZ[:, :], xT[:, c, :], U[:, c, :], start=(first and c == 0),
                                            stop=(not first and c == DC - 1))
                last.then_inc(z_added, 1)

            def query_key(n, st=OWN):
                xT, qf, _, _ = stage[st]
                pX = stage_ps[st]
                for c in range(DC):
                    last = nc.tensor.matmul(pX[:, 0, :], w13[:, c, :], xT[:, c, :], start=(c == 0), stop=(c == DC - 1))
                last.then_inc(qk_made, 1)
                pe.wait_ge(qf_made, n + 1)
                nc.tensor.matmul(pX[:, 1, :], w2, qf, start=True, stop=True).then_inc(q2_made, 1)

            def turn_h(i, par):
                pe.wait_ge(h_made, i + 1)
                pe.wait_ge(q2_taken, i + 1)
                turn_x(XN[par], par)

            def phase0(i, j, par, last):
                if not last:
                    turn_h(i + 1, 1 - par)
                pe.wait_ge(xT_made, i + 1)
                query_key(i, par)

            turn_h(0, 0)
            tiles(pe, phase0)

            def logits(s, i, j, par):
                g = s * T + i
                pe.wait_ge(q_in[par], 16 * (s * (T // 2) + j + 1))
                for c in range(NCH):
                    w = min(CHUNK, NP - c * CHUNK)
                    pe.wait_ge(logits_taken, g * NCH + c + 1)
                    for a, K in enumerate((K12, K12, K13)):
                        last = nc.tensor.matmul(pL[(par + c) % 2][:, 0:w], qs[par][:, a, :], K[:, c * CHUNK:c * CHUNK + w],
                                                start=(a == 0), stop=(a == 2))
                    last.then_inc(logits_made, 1)

            def turn(s, i, par, q, src):
                n, _, bank, _ = group(s, i, par, q)
                pe.wait_ge(lo_left, n + 1)
                for b in blocks[q % NG]:
                    last = nc.tensor.matmul(pT[bank][:, b % GB, :], src[:, b * P:(b + 1) * P], ident[:, :],
                                            is_transpose=True, start=(b % GB == 0), stop=False, skip_group_check=True)
                last.then_inc(turned, 1)

            def take_hi(s, i, par, q):
                n, slot, bank, _ = group(s, i, par, q)
                m = len(blocks[q % NG])
                pe.wait_ge(hi_made, n + 1)
                nc.tensor.matmul(pT[bank][:, 0:m, :], minus_eye[:, :], ring[slot][:, 0:m, 0:P],
                                 start=False, stop=True, skip_group_check=True).then_inc(hi_taken, 1)

            def products(acc, weights, X, k, done):
                for b in blocks[k]:
                    whi, wlo = weights(b)
                    xhi, xlo = X[:, b, 0:D], X[:, b, D:2 * D]
                    nc.tensor.matmul(acc[:, :], whi, xhi, start=(b == 0), stop=False)
                    nc.tensor.matmul(acc[:, :], whi, xlo, start=False, stop=False)
                    last = nc.tensor.matmul(acc[:, :], wlo, xhi, start=False, stop=(b == T - 1))
                if done is not None:
                    last.then_inc(done, 1)

            def turn_Xf_of(i):
                pe.wait_ge(xnR_made, i + 2)
                pe.wait_ge(q2_taken, T + i + 3)
                turn_x(XN[0])

            def tile(s, i, j, par, first):
                g = s * T + i
                more = has_more(i)
                for q in range(L[s] + 2):
                    if q < L[s]:
                        if q == 0:
                            pe.wait_ge(mask_made, g + 1)
                        if q == NG:
                            pe.wait_ge(adj_scaled, 2 * (i + 1))
                        turn(s, i, par, q, E[par] if q < NG else AD)
                    if 1 <= q <= L[s]:
                        take_hi(s, i, par, q - 1)
                    if q >= 2:
                        n, slot, _, _ = group(s, i, par, q - 2)
                        of_A = q - 2 < NG
                        if q == 2 or q - 2 == NG:
                            pe.wait_ge(xnA_made if of_A else xnR_made, g + 1)
                        if s == 0 and q == 2 and not first:
                            add_z(T + 2 * (i - 1) + 1, U1, False)
                        pe.wait_ge(lo_left, n + 3)
                        products(pA if of_A else pR, lambda b: (ring[slot][:, b % GB, 0:P], ring[slot][:, b % GB, P:2 * P]),
                                 XA, (q - 2) % NG, used)
                    if s == 0:
                        if q == 1 and not first:
                            turn_Xf_of(i - 1)
                        if q == NG + 1 and more:
                            logits(s, i + 2, j + 1, par)
                        if q == NG + 2:
                            pe.wait_ge(xnA_made, g + 2)
                            turn_x(XN[1])
                        if q == NG + 3:
                            pe.wait_ge(z_taken, g + 1)
                            add_z(T + 2 * g, U2, True)
                            query_key(T + i)
                if s == 1:
                    if more:
                        logits(s, i + 2, j + 1, par)
                    pe.wait_ge(xnA_made, g + 2)
                    turn_x(XN[1])
                    pe.wait_ge(rt_in, 16 * (i + 1))
                    pe.wait_ge(xnR_made, g + 1)
                    for k in range(NG):
                        products(pR, lambda b: (RT[:, b, 0:P], RT[:, b, P:2 * P]), XB, k, RT_used if k == NG - 1 else None)
                    pe.wait_ge(z_taken, g + 1)
                    add_z(T + 2 * g, U2, True)
                    pe.wait_ge(xnR_made, g + 2)
                    turn_x(XN[0])
                    add_z(T + 2 * g + 1, U1, False)

            for s in range(2):
                pe.wait_ge(k_in, 64 * (s + 1))
                pe.wait_ge(U_in, 32)
                logits(s, 0, 0, 0)
                logits(s, 1, 0, 1)
                if s == 1:
                    pe.wait_ge(xa_in, 32)
                    pe.wait_ge(U_in, 16 * 4)
                    pe.wait_ge(lo_made, 3 * T)
                if s == 0:
                    tiles_after_first(pe, lambda i, j, par, first: tile(0, i, j, par, first))
                    turn_Xf_of(T - 1)
                    add_z(T + 2 * (T - 1) + 1, U1, False)
                else:
                    tiles(pe, lambda i, j, par, last: tile(1, i, j, par, False))


_INS = ["x", "adj", "L0_gnn_W1", "L0_gnn_W2", "L0_gnn_W3", "L0_gnn_U1_0", "L0_gnn_U1_1", "L0_gnn_U2_0", "L0_gnn_U2_1",
        "L0_gnn_gamma", "L0_gnn_beta"]


def kernel(**inputs):
    import numpy as _np
    import concourse.bacc as _bacc
    from concourse import mybir as _mybir
    from concourse.bass_utils import run_bass_kernel_spmd as _run

    nc = _bacc.Bacc("TRN2", target_bir_lowering=False, num_devices=1)
    arrays, args = {}, []
    for name in _INS:
        a = _np.ascontiguousarray(inputs[name])
        arrays[f"in_{name}_dram"] = a
        args.append(nc.dram_tensor(f"in_{name}_dram", a.shape, _mybir.dt.from_np(a.dtype), kind="ExternalInput").ap())
    shape = inputs["x"].shape
    args.append(nc.dram_tensor("out_dram", shape, _mybir.dt.float32, kind="ExternalOutput").ap())
    build_top_p_gnn(nc, *args)
    r = _run(nc, [arrays], core_ids=[0])
    return r.results[0]["out_dram"]
```
